# Optimizing a Trainium2 kernel written in Bass

```python
import numpy as np
import jax
import jax.numpy as jnp

def _softmax(x, axis=-1):
    return jax.nn.softmax(x, axis=axis)
def _gelu(x):
    return jax.nn.gelu(x, approximate=True)
def _silu(x):
    return jax.nn.silu(x)
def _sigmoid(x):
    return jax.nn.sigmoid(x)
def _layernorm(x, axis=-1, eps=1e-5):
    m = jnp.mean(x, axis=axis, keepdims=True)
    v = jnp.var(x, axis=axis, keepdims=True)
    return (x - m) / jnp.sqrt(v + eps)
def _scatter_add(tgt, idx, src, axis=0):
    return tgt.at[idx].add(src)
def _segment_sum(src, seg, n):
    return jax.ops.segment_sum(src, seg, n)

kernel_name = 'mk_adj_ffn_d1_adj_256_1a0b75'

def setup_inputs(seed: int = 0):
    np.random.seed(seed)
    _w = jnp.asarray
    def _rec_inputs():
        import jax
        import jax.numpy as jnp
        _gk = jax.random.key(seed)
        x = -0.0005207 + 1.001 * jax.random.normal(jax.random.fold_in(_gk, 1), (8192, 256), jnp.float32)
        _w = (1.0 + jnp.arange(8192, dtype=jnp.float32)) ** -0.5
        _w = _w / _w.mean()
        _pij = jnp.clip(0.000488281 * _w[:, None] * _w[None, :], 0.0, 1.0)
        _a = jax.random.uniform(jax.random.fold_in(_gk, 2), (8192, 8192)) < _pij
        _af = _a.astype(jnp.float32)
        adj = _af
        return x, adj
    x, adj = _rec_inputs()
    def _L0_gnn_setup():
        import jax, jax.numpy as jnp
        import numpy as np
        NEG = -9000000000000000.0
        key = jax.random.key(seed)
        k1, k2, k3, k4 = jax.random.split(key, 4)
        N, Fin, Fout = (8192, 256, 256)
        h = jax.random.normal(k1, (N, Fin), dtype=jnp.float32)
        adj = jax.random.randint(k2, (N, N), 0, 2).astype(jnp.float32)
        W = jax.random.normal(k3, (Fin, Fout), dtype=jnp.float32) * (1.414 * np.sqrt(2.0 / (Fin + Fout)))
        a = jax.random.normal(k4, (2 * Fout, 1), dtype=jnp.float32) * (1.414 * np.sqrt(2.0 / (2 * Fout + 1)))
        return {'h': h, 'adj': adj, 'W': W, 'a': a}
    _L0_gnn_all = _L0_gnn_setup()
    _L0_gnn_in = {k: v for k, v in _L0_gnn_all.items() if k in ('W', 'a', )}
    del _L0_gnn_all

    def _L0_ffn_setup():
        import jax, jax.numpy as jnp
        import numpy as np
        B, T, D, H, L = (16, 4096, 256, 256, 2)

        def _lstm(x, W_ih, W_hh, b_ih, b_hh):
            x_proj = jnp.einsum('btd,gd->btg', x, W_ih) + b_ih + b_hh
            h0 = jnp.zeros((x.shape[0], W_hh.shape[1]), x.dtype)
            c0 = jnp.zeros_like(h0)

            def step(carry, xp):
                h, c = carry
                gates = xp + h @ W_hh.T
                i, f, g, o = jnp.split(gates, 4, axis=-1)
                c = jax.nn.sigmoid(f) * c + jax.nn.sigmoid(i) * jnp.tanh(g)
                h = jax.nn.sigmoid(o) * jnp.tanh(c)
                return ((h, c), h)
            _, hs = jax.lax.scan(step, (h0, c0), jnp.swapaxes(x_proj, 0, 1))
            return jnp.swapaxes(hs, 0, 1)
        key = jax.random.key(seed)
        ks = jax.random.split(key, 9)
        s = 1.0 / np.sqrt(H)
        u = lambda k, shape: jax.random.uniform(k, shape, jnp.float32, -s, s)
        return {'x': jax.random.normal(ks[0], (B, T, D), jnp.float32), 'W_ih': u(ks[1], (4 * H, D)), 'W_hh': u(ks[2], (4 * H, H)), 'b_ih': u(ks[3], (4 * H,)), 'b_hh': u(ks[4], (4 * H,)), 'W_lin': u(ks[5], (L, H)), 'b_lin': u(ks[6], (L,)), 'fw_att': jnp.full((1, H), 0.001, jnp.float32), 'bw_att': jnp.full((1, H), 0.001, jnp.float32)}
    _L0_ffn_all = _L0_ffn_setup()
    _L0_ffn_in = {k: v for k, v in _L0_ffn_all.items() if k in ('W_ih', 'W_hh', 'b_ih', 'b_hh', 'W_lin', 'b_lin', 'fw_att', 'bw_att', )}
    del _L0_ffn_all

    return {
        "x": x,
        "adj": adj,
        "L0_gnn_W": _L0_gnn_in["W"],
        "L0_gnn_a": _L0_gnn_in["a"],
        "L0_ffn_W_ih": _L0_ffn_in["W_ih"],
        "L0_ffn_W_hh": _L0_ffn_in["W_hh"],
        "L0_ffn_b_ih": _L0_ffn_in["b_ih"],
        "L0_ffn_b_hh": _L0_ffn_in["b_hh"],
        "L0_ffn_W_lin": _L0_ffn_in["W_lin"],
        "L0_ffn_b_lin": _L0_ffn_in["b_lin"],
        "L0_ffn_fw_att": _L0_ffn_in["fw_att"],
        "L0_ffn_bw_att": _L0_ffn_in["bw_att"],
    }

def reference(x, adj, L0_gnn_W, L0_gnn_a, L0_ffn_W_ih, L0_ffn_W_hh, L0_ffn_b_ih, L0_ffn_b_hh, L0_ffn_W_lin, L0_ffn_b_lin, L0_ffn_fw_att, L0_ffn_bw_att):
    import jax
    import jax.numpy as jnp
    def _L0_gnn_ref(h, adj, W, a):
        import jax, jax.numpy as jnp
        import numpy as np
        NEG = -9000000000000000.0
        Fout = W.shape[1]
        Wh = h @ W
        Wh1 = Wh @ a[:Fout, :]
        Wh2 = Wh @ a[Fout:, :]
        e = jax.nn.leaky_relu(Wh1 + Wh2.T, 0.2)
        mask = (adj > 0).astype(e.dtype)
        e = e * mask + NEG * (1.0 - mask)
        attention = jax.nn.softmax(e, axis=1)
        h_prime = attention @ Wh
        return jax.nn.elu(h_prime)

    def _L0_ffn_ref(x, W_ih, W_hh, b_ih, b_hh, W_lin, b_lin, fw_att, bw_att):
        import jax, jax.numpy as jnp
        import numpy as np
        B, T, D, H, L = (16, 4096, 256, 256, 2)

        def _lstm(x, W_ih, W_hh, b_ih, b_hh):
            x_proj = jnp.einsum('btd,gd->btg', x, W_ih) + b_ih + b_hh
            h0 = jnp.zeros((x.shape[0], W_hh.shape[1]), x.dtype)
            c0 = jnp.zeros_like(h0)

            def step(carry, xp):
                h, c = carry
                gates = xp + h @ W_hh.T
                i, f, g, o = jnp.split(gates, 4, axis=-1)
                c = jax.nn.sigmoid(f) * c + jax.nn.sigmoid(i) * jnp.tanh(g)
                h = jax.nn.sigmoid(o) * jnp.tanh(c)
                return ((h, c), h)
            _, hs = jax.lax.scan(step, (h0, c0), jnp.swapaxes(x_proj, 0, 1))
            return jnp.swapaxes(hs, 0, 1)
        lstm_out = _lstm(x, W_ih, W_hh, b_ih, b_hh)
        logits = jnp.einsum('bth,lh->btl', lstm_out, W_lin) + b_lin
        g = jax.lax.stop_gradient(jnp.argmax(logits, axis=-1).astype(lstm_out.dtype))[..., None]
        w = g * lstm_out
        inc = jnp.cumsum(w, axis=1)
        prefix = inc - w
        suffix = inc[:, -1:, :] - inc
        return 2.0 * lstm_out + prefix * fw_att + suffix * bw_att

    x = x + _L0_gnn_ref(_layernorm(x, axis=-1), adj, L0_gnn_W, L0_gnn_a)
    x = x + _L0_ffn_ref((_layernorm(x, axis=-1))[None], L0_ffn_W_ih, L0_ffn_W_hh, L0_ffn_b_ih, L0_ffn_b_hh, L0_ffn_W_lin, L0_ffn_b_lin, L0_ffn_fw_att, L0_ffn_bw_att)[0]
    return x


_drawn_inputs = setup_inputs


def setup_inputs(seed=0):
    import zlib

    import numpy as np

    out = dict(_drawn_inputs(seed))
    spreads = {'L0_ffn_fw_att': (0.0010000000474974513, 0.2),
     'L0_ffn_bw_att': (0.0010000000474974513, 0.2)}
    factors = {}
    for name, (base, spread) in spreads.items():
        noise = np.random.default_rng([zlib.crc32(name.encode()), seed]).standard_normal(out[name].shape)
        drawn = base * np.exp(spread * noise) if base else spread * noise
        out[name] = jnp.asarray(drawn.astype(out[name].dtype))
    for name, factor in factors.items():
        out[name] = (out[name] * factor).astype(out[name].dtype)
    return out
```

```python
from contextlib import ExitStack

import concourse.bass as bass
from concourse import mybir

F32 = mybir.dt.float32
BF16 = mybir.dt.bfloat16
I32 = mybir.dt.int32
ALU = mybir.AluOpType
ACT = mybir.ActivationFunctionType
AX = mybir.AxisListType

P = 128
D = 256
KD = D // P
G4 = 4 * D
HALF = G4 // 2
EPS = 1e-5
SLOPE = 0.2
TOL = 2.0 ** -19
CHUNK = 2048
PIECE = 1024
GROUP = 512
E_SLOTS = 4


def adj_ffn_kernel(nc, x, adj, w_gnn, a_pair, w_ih_t, w_hh_t, b_ih, b_hh, w_lin_t, b_lin, fw, bw, out, warm=32, SWEEPS=P - 1):
    N = x.shape[0]
    L = N // P
    NCH, NP, NG = N // CHUNK, N // PIECE, N // GROUP
    BPG = GROUP // P
    GPP = PIECE // GROUP
    WARM = warm
    OFF = L - WARM

    x_kl = x.rearrange("(k l) d -> k l d", l=L)
    adj_kl = adj.rearrange("(k l) j -> k l j", l=L)
    out_kl = out.rearrange("(k l) d -> k l d", l=L)
    t_line = nc.dram_tensor("t_line", [N], F32, kind="Internal").ap()
    s_line = nc.dram_tensor("s_line", [N], F32, kind="Internal").ap()
    xp_dram = nc.dram_tensor("xp_dram", [P, L, G4], F32, kind="Internal").ap()
    x1_dram = nc.dram_tensor("x1_dram", [P, L, D], F32, kind="Internal").ap()
    end_dram = nc.dram_tensor("end_dram", [2, P, D], F32, kind="Internal").ap()
    base_dram = nc.dram_tensor("base_dram", [P, L, D], F32, kind="Internal").ap()

    with ExitStack() as ctx:
        def sb(name, shape, dt=F32):
            return ctx.enter_context(nc.sbuf_tensor(name, shape, dt))

        def pb(name):
            return ctx.enter_context(nc.psum_tensor(name, [P, 512], F32))

        def sem(name):
            return ctx.enter_context(nc.semaphore(name))

        def hold(eng):
            eng.sem_inc(held, 1)

        wh = sb("wh", [P, L, D])
        t_row = sb("t_row", [P, N])
        adj_sb = sb("adj_sb", [P, 2, CHUNK])
        nb = sb("nb", [P, 2, N], BF16)
        E = sb("E", [P, E_SLOTS, PIECE])
        PT = sb("PT", [P, 2, GROUP])
        wih = sb("wih", [P, KD, G4])
        whh = sb("whh", [P, KD, G4])
        bias = sb("bias", [P, G4])
        xp = sb("xp", [P, G4])
        ident = sb("ident", [P, P])
        shift = sb("shift", [P, P])
        w1b = sb("w1b", [P, D])
        w3 = sb("w3", [P, D])
        small = sb("small", [P, 64])
        x_in = sb("x_in", [P, 2, D])
        x1 = sb("x1", [P, D])
        w1 = sb("w1", [P, D])
        w2 = sb("w2", [P, D])
        xn = sb("xn", [P, D])
        xnT = sb("xnT", [P, KD, P])
        hT = sb("hT", [P, KD, P])
        c2 = sb("c2", [P, D])
        h2 = sb("h2", [P, D])
        csum = sb("csum", [P, D])
        S2 = sb("S2", [P, 2, D])
        fb = sb("fb", [P, 2, D])
        base = sb("base", [P, D])
        s_perm = sb("s_perm", [P, L])
        wl = sb("wl", [P, KD, 2])
        rs = sb("rs", [P, 2, NP])
        gmx = sb("gmx", [P, 2, NCH])
        flag = sb("flag", [P, 2], I32)

        ps_t = [pb("ps_t0"), pb("ps_t1")]
        ps_o = [pb("ps_o0"), pb("ps_o1")]
        ps_x, ps_h = pb("ps_x"), pb("ps_h")
        ps_g = [pb("ps_g0"), pb("ps_g1")]

        def col(k, n=1):
            return small[:, k:k + n]
        BL, TMIN, MHALF = col(0, 2), col(2), col(3)
        BIAS1 = [col(4), col(5)]
        BIAS2 = [col(6), col(7)]
        GM = [col(8), col(9)]
        Z1, Z2, Z3, SC, NEGM = col(10), col(11), col(12), col(34), col(35)
        RSUM, NONE, DEN, RINV = col(13), col(14), col(15), col(16)
        STATS, MV, VE, RSTD = col(17, 6), col(23, 2), col(25), col(26)
        LD, LG = col(27), col(28)
        PAD = col(29)
        DMX = col(30, 4)

        x_all = wh
        strict = E[:, 0, 0:P]
        w_sb = E[:, 1, 0:KD * D].rearrange("p (k d) -> p k d", k=KD)
        a_row = E[:, 2, 0:2 * D].rearrange("p (k d) -> p k d", k=2)
        ones = E[:, 3, 0:P]
        stat_all = nb[:, 0, 0:16 * L].bitcast(F32)
        mv_all = nb[:, 0, 16 * L:20 * L].bitcast(F32)
        rstd_all = nb[:, 0, 20 * L:22 * L].bitcast(F32)
        half_all = nb[:, 0, 22 * L:24 * L].bitcast(F32)
        hn = adj_sb[:, :, 0:D]
        hnT = adj_sb[:, :, D:2 * D].rearrange("p u (k q) -> p u k q", k=KD)
        dump = adj_sb[:, :, 2 * D:3 * D]
        xp_again = [nb[:, u, 0:2 * G4].bitcast(F32) for u in range(2)]
        x1_again = [nb[:, u, 2 * G4:2 * G4 + 2 * D].bitcast(F32) for u in range(2)]
        st_cols = base[:, 0:2 * L].rearrange("p (a b) -> p a b", a=2)
        st_out = w1[:, :].rearrange("p (a b) -> p a b", a=2)

        XL = 8
        XB = L // XL
        x_loaded = [sem(f"x_loaded{i}") for i in range(XL)]
        w_loaded, row_loaded = sem("w_loaded"), sem("row_loaded")
        consts = sem("consts")
        st_done, ag_done = sem("st_done"), sem("ag_done")
        rs_done, rs_in = sem("rs_done"), sem("rs_in")
        hn_ready, hnT_mm, hnT_ready = sem("hn_ready"), sem("hnT_mm"), sem("hnT_ready")
        wh_mm, wh_ready, st_ready = sem("wh_mm"), sem("wh_ready"), sem("st_ready")
        cs_mm, stT_mm, stT_ready = sem("cs_mm"), sem("stT_mm"), sem("stT_ready")
        line_stored, line_loaded = sem("line_stored"), sem("line_loaded")
        prep, tmin_ready = sem("prep"), sem("tmin_ready")
        held = sem("held")
        prep2, bias_sum = sem("prep2"), sem("bias_sum")

        with nc.Block() as block:
            @block.sync
            def _(sp):
                for i in range(XL):
                    sp.dma_start(x_all[:, i * XB:(i + 1) * XB, :],
                                 x[i * XB * P:(i + 1) * XB * P, :].rearrange("(b p) d -> p b d", p=P)
                                 ).then_inc(x_loaded[i], 16)
                sp.wait_ge(stT_ready, 1)
                for i, line in enumerate((s_line, t_line)):
                    sp.dma_start(line.rearrange("(b p) -> b p", p=P), st_out[0:L, i, :]).then_inc(line_stored, 16)
                sp.wait_ge(line_stored, 32)
                sp.dma_start(t_row[:, :], t_line.rearrange("(o n) -> o n", o=1).to_broadcast([P, N])).then_inc(line_loaded, 16)
                s_kl = s_line.rearrange("(k l) -> k l", l=L)
                sp.dma_start(s_perm[:, 0:WARM], s_kl[:, OFF:L]).then_inc(line_loaded, 16)
                sp.dma_start(s_perm[:, WARM:L], s_kl[:, 0:OFF]).then_inc(line_loaded, 16)

            @block.scalar
            def _(act):
                act.dma_start(w_sb, w_gnn.rearrange("(k p) d -> p k d", p=P)).then_inc(w_loaded, 16)
                act.dma_start(a_row, a_pair.rearrange("(o a d) c -> o a (d c)", o=1, a=2).to_broadcast([P, 2, D])).then_inc(w_loaded, 16)
                act.dma_start(wih[:, :, :], w_ih_t.rearrange("(k p) g -> p k g", p=P)).then_inc(row_loaded, 16)
                act.dma_start(whh[:, :, :], w_hh_t.rearrange("(k p) g -> p k g", p=P)).then_inc(row_loaded, 16)
                act.dma_start(bias[:, :], b_ih.rearrange("(o g) -> o g", o=1).to_broadcast([P, G4])).then_inc(row_loaded, 16)
                act.dma_start(t_row[:, 0:G4], b_hh.rearrange("(o g) -> o g", o=1).to_broadcast([P, G4])).then_inc(row_loaded, 16)
                act.dma_start(fb[:, 0, :], fw.to_broadcast([P, D])).then_inc(row_loaded, 16)
                act.dma_start(fb[:, 1, :], bw.to_broadcast([P, D])).then_inc(row_loaded, 16)
                act.dma_start(BL, b_lin.rearrange("(o g) -> o g", o=1).to_broadcast([P, 2])).then_inc(row_loaded, 16)
                act.dma_start(wl[:, :, :], w_lin_t.rearrange("(k p) g -> p k g", p=P)).then_inc(row_loaded, 16)
                with act.Fori(0, L // 2) as i:
                    for u in range(2):
                        act.wait_ge(hnT_mm, 2 * i + u + 1)
                        nc.scalar.copy(hnT[:, u, :, :].rearrange("p k q -> p (k q)"), ps_t[u][:, 0:D]).then_inc(hnT_ready, 1)

            @block.gpsimd
            def _(pool):
                nc.gpsimd.memset(ones, 1.0).then_inc(consts, 1)
                nc.gpsimd.memset(ident[:, :], 1.0).then_inc(consts, 1)
                nc.gpsimd.memset(MHALF, -0.5).then_inc(consts, 1)
                nc.gpsimd.memset(half_all, -0.5).then_inc(consts, 1)
                pool.wait_ge(consts, 4)
                nc.gpsimd.affine_select(out=ident[:, :], in_=ident[:, :], compare_op=ALU.is_equal, fill=0.0,
                                        base=0, pattern=[[-1, P]], channel_multiplier=1).then_inc(consts, 1)
                pool.wait_ge(rs_in, 1)
                nc.gpsimd.tensor_tensor(rstd_all, rstd_all, half_all, ALU.pow).then_inc(rs_done, 1)

            @block.vector
            def _(dve):
                for b in range(L):
                    if b % XB == 0:
                        dve.wait_ge(x_loaded[b // XB], 16)
                    nc.vector.bn_stats(stat_all[:, 6 * b:6 * b + 6], x_all[:, b, :]).then_inc(st_done, 1)
                for b in range(L):
                    dve.wait_ge(st_done, b + 1)
                    nc.vector.bn_aggr(mv_all[:, 2 * b:2 * b + 2], stat_all[:, 6 * b:6 * b + 6]).then_inc(ag_done, 1)
                dve.wait_ge(ag_done, L)
                dve.wait_ge(consts, 5)
                nc.vector.tensor_scalar(rstd_all, mv_all.rearrange("p (b c) -> p b c", c=2)[:, :, 1], EPS, None,
                                        ALU.add).then_inc(rs_in, 1)
                dve.wait_ge(rs_done, 1)
                def norm(b, u):
                    nc.vector.tensor_copy(col(40 + 2 * u), mv_all[:, bass.ds(2 * b, 1)])
                    nc.vector.tensor_copy(col(41 + 2 * u), rstd_all[:, bass.ds(b, 1)]).then_inc(prep, 1)
                    dve.wait_ge(prep, b + 1)
                    hold(dve)
                    nc.vector.tensor_scalar(hn[:, u, :], x_all[:, bass.ds(b, 1), :].rearrange("p o d -> p (o d)"),
                                            col(40 + 2 * u), col(41 + 2 * u), ALU.subtract, ALU.mult).then_inc(hn_ready, 1)

                def take(b, u):
                    dve.wait_ge(wh_mm, b + 1)
                    hold(dve)
                    w_b = wh[:, bass.ds(b, 1), :].rearrange("p o d -> p (o d)")
                    nc.vector.tensor_copy(w_b, ps_o[u][:, 0:D]).then_inc(wh_ready, 1)
                    dve.wait_ge(wh_ready, b + 1)
                    for k in range(2):
                        nc.vector.scalar_tensor_tensor(out=dump[:, k, :], in0=w_b, scalar=1.0, in1=a_row[:, k, :],
                                                       op0=ALU.mult, op1=ALU.mult, accum_out=col(44 + k)).then_inc(st_ready, 1)
                    dve.wait_ge(st_ready, 2 * b + 2)
                    hold(dve)
                    nc.vector.tensor_copy(st_cols[:, :, bass.ds(b, 1)].rearrange("p a o -> p (a o)"), col(44, 2)).then_inc(prep2, 1)

                norm(0, 0)
                dve.wait_ge(w_loaded, 32)
                with dve.Fori(0, L // 2 - 1) as i:
                    norm(2 * i + 1, 1)
                    take(2 * i, 0)
                    norm(2 * i + 2, 0)
                    take(2 * i + 1, 1)
                norm(L - 1, 1)
                take(L - 2, 0)
                take(L - 1, 1)
                dve.wait_ge(row_loaded, 8 * 16)
                for t, scale in ((wih, 1.0), (whh, 0.5)):
                    for lo, hi, f in ((0, 2 * D, 0.5), (2 * D, 3 * D, 1.0), (3 * D, G4, 0.5)):
                        if scale * f != 1.0:
                            nc.vector.tensor_scalar(t[:, :, lo:hi], t[:, :, lo:hi], scale * f, None, ALU.mult)
                nc.vector.tensor_scalar(wl[:, :, :], wl[:, :, :], 0.5, None, ALU.mult)
                nc.vector.tensor_scalar(fb[:, :, :], fb[:, :, :], 0.5, None, ALU.mult)
                nc.vector.tensor_tensor(bias[:, :], bias[:, :], t_row[:, 0:G4], ALU.add).then_inc(bias_sum, 1)
                dve.wait_ge(bias_sum, 1)
                nc.vector.tensor_scalar(bias[:, 0:2 * D], bias[:, 0:2 * D], 0.5, None, ALU.mult)
                nc.vector.tensor_scalar(bias[:, 3 * D:G4], bias[:, 3 * D:G4], 0.5, None, ALU.mult)
                nc.vector.memset(hT[:, :, :], 0.0)
                nc.vector.memset(c2[:, :], 0.0)
                nc.vector.memset(S2[:, :, :], 0.0)
                dve.wait_ge(cs_mm, 1)
                nc.vector.tensor_copy(csum[:, :], ps_g[0][:, 0:D])
                dve.wait_ge(stT_mm, 1)
                nc.vector.tensor_copy(st_out[0:L, :, :], ps_h[0:L, 0:2 * P].rearrange("p (a b) -> p a b", a=2)).then_inc(stT_ready, 1)
                dve.wait_ge(line_loaded, 48)
                nc.vector.tensor_reduce(out=TMIN, in_=t_row[:, :], axis=AX.X, op=ALU.min).then_inc(tmin_ready, 1)
                dve.wait_ge(tmin_ready, 1)
                nc.vector.tensor_scalar(t_row[:, :], t_row[:, :], TMIN, 1.0, ALU.subtract, ALU.add)
                nc.vector.tensor_scalar(s_perm[:, :], s_perm[:, :], TMIN, -1.0, ALU.add, ALU.add)

            @block.tensor
            def _(pe):
                pe.wait_ge(consts, 5)
                pe.wait_ge(w_loaded, 32)

                def turn(b, u):
                    pe.wait_ge(hn_ready, b + 1)
                    for k in range(KD):
                        last = nc.tensor.transpose(ps_t[u][:, k * P:(k + 1) * P], hn[:, u, k * P:(k + 1) * P], ident[:, :])
                    last.then_inc(hnT_mm, 1)

                def product(b, u, first, final):
                    pe.wait_ge(hnT_ready, b + 1)
                    for k in range(KD):
                        last = nc.tensor.matmul(ps_o[u][:, 0:D], hnT[:, u, k, :], w_sb[:, k, :], start=k == 0, stop=k == KD - 1)
                    last.then_inc(wh_mm, 1)

                def column_sum(b, first, final):
                    pe.wait_ge(wh_ready, b + 1)
                    last = nc.tensor.matmul(ps_g[0][:, 0:D], ones, wh[:, bass.ds(b, 1), :].rearrange("p o d -> p (o d)"),
                                            start=first, stop=final)
                    if final:
                        last.then_inc(cs_mm, 1)

                turn(0, 0)
                product(0, 0, True, False)
                turn(1, 1)
                product(1, 1, False, False)
                column_sum(0, True, False)
                with pe.Fori(0, L // 2 - 1) as i:
                    turn(2 * i + 2, 0)
                    product(2 * i + 2, 0, False, False)
                    column_sum(2 * i + 1, False, False)
                    turn(2 * i + 3, 1)
                    product(2 * i + 3, 1, False, False)
                    column_sum(2 * i + 2, False, False)
                column_sum(L - 1, False, True)
                pe.wait_ge(prep2, L)
                for k in range(2):
                    last = nc.tensor.transpose(ps_h[0:L, k * P:(k + 1) * P], st_cols[:, k, :], ident[:, :])
                last.then_inc(stT_mm, 1)


        adj_loaded = [sem("adj_loaded0"), sem("adj_loaded1")]
        xi_loaded = [sem("xi_loaded0"), sem("xi_loaded1")]
        guard_done, guard_max = sem("guard_done"), sem("guard_max")
        y_ready, y_sum, e_ready, p_ready = sem("y_ready"), sem("y_sum"), sem("e_ready"), sem("p_ready")
        turned, pt_ready, acc_ready = sem("turned"), sem("pt_ready"), sem("acc_ready")
        fin, elu_ready, rstd_ready, x1_stored = sem("fin"), sem("elu_ready"), sem("rstd_ready"), sem("x1_stored")
        xnT_mm, xnT_ready = sem("xnT_mm"), sem("xnT_ready")
        in_mm, in_ready, in_stored = sem("in_mm"), sem("in_ready"), sem("in_stored")
        rec_mm, gate_sum, gate_act = sem("rec_mm"), sem("gate_sum"), sem("gate_act")
        cell, cell_act, h_ready = sem("cell"), sem("cell_act"), sem("h_ready")
        hT_mm, hT_ready = sem("hT_mm"), sem("hT_ready")
        logit_mm, picked = sem("logit_mm"), sem("picked")
        part_a, base_ready, base_stored = sem("part_a"), sem("base_ready"), sem("base_stored")
        shift_mm, shifted, shifted_h = sem("shift_mm"), sem("shifted"), sem("shifted_h")
        again_in = [sem("again_in0"), sem("again_in1")]
        shift_made, end_stored = sem("shift_made"), sem("end_stored")
        x1_free = sem("x1_free")
        FIN = 16
        LEAD = 2

        def at(n, per, k):
            return n * per + k

        def tiles(eng, body):
            body(0, 0, True, None)
            with eng.Fori(0, WARM // 2) as i:
                for u in range(2):
                    body(2 * i + 1 + u, (1 + u) % 2, True, "warm")
            yield
            with eng.Fori(0, (L - 2 - WARM) // 2) as i:
                for u in range(2):
                    body(2 * i + WARM + 1 + u, (1 + u) % 2, True, "main")
            body(L - 1, (L - 1) % 2, False, "main")

        with nc.Block() as block:
            @block.sync
            def _(sp):
                def load(n, position, u, first=False):
                    for c in range(NCH):
                        if not (first and c < 2):
                            sp.wait_ge(guard_done, at(n, NCH, c - 1))
                        sp.dma_start(adj_sb[:, c % 2, :],
                                     adj_kl[:, bass.ds(position, 1), c * CHUNK:(c + 1) * CHUNK].rearrange("k o j -> k (o j)")
                                     ).then_inc(adj_loaded[c % 2], 16)
                    if not first:
                        sp.wait_ge(fin, FIN * n - (2 * FIN - 8))
                    sp.dma_start(x_in[:, u, :], x_kl[:, bass.ds(position, 1), :].rearrange("k o d -> k (o d)")).then_inc(xi_loaded[u], 16)

                load(0, OFF, 0, True)
                for c in range(NCH):
                    sp.wait_ge(guard_done, NCH + c - 1)
                    sp.dma_start(adj_sb[:, c % 2, :], adj_kl[:, OFF + 1, c * CHUNK:(c + 1) * CHUNK]).then_inc(adj_loaded[c % 2], 16)
                sp.dma_start(x_in[:, 1, :], x_kl[:, OFF + 1, :]).then_inc(xi_loaded[1], 16)
                with sp.Fori(0, WARM // 2 - 1) as i:
                    for u in range(2):
                        load(2 * i + 2 + u, 2 * i + (OFF + 2 + u), u)
                with sp.Fori(0, (L - WARM) // 2) as i:
                    for u in range(2):
                        load(2 * i + WARM + u, 2 * i + u, u)
                sp.wait_ge(p_ready, NP * L)
                sp.wait_ge(in_stored, 16 * L)
                sp.wait_ge(x1_stored, 16 * L)
                for r in range(WARM):
                    if r >= 2:
                        sp.wait_ge(h_ready, L + r - 1)
                        sp.wait_ge(base_ready, L + r - WARM)
                    sp.dma_start(xp_again[r % 2], xp_dram[:, OFF + r, :]).then_inc(again_in[r % 2], 16)
                    sp.dma_start(x1_again[r % 2], x1_dram[:, OFF + r, :]).then_inc(again_in[r % 2], 16)

            @block.gpsimd
            def _(pool):
                pool.sem_inc(x1_free, 1)
                pool.sem_inc(base_ready, 1)
                pool.sem_inc(gate_sum, 2)
                pool.sem_inc(hT_ready, 1)
                pool.sem_inc(picked, 3)
                nc.gpsimd.memset(shift[:, :], 1.0).then_inc(shift_made, 1)
                pool.wait_ge(shift_made, 1)
                nc.gpsimd.affine_select(out=shift[:, :], in_=shift[:, :], compare_op=ALU.is_equal, fill=0.0,
                                        base=1, pattern=[[-1, P]], channel_multiplier=1).then_inc(shift_made, 1)

                def finish_x(m, position):
                    pool.wait_ge(fin, at(m, FIN, 12))
                    hold(pool)
                    pool.dma_start(x1_dram[:, bass.ds(position, 1), :].rearrange("k o d -> k (o d)"), x1[:, :]).then_inc(x1_stored, 16)

                def finish_rstd(m):
                    pool.wait_ge(fin, at(m, FIN, 15))
                    nc.gpsimd.tensor_tensor(RSTD, VE, MHALF, ALU.pow).then_inc(rstd_ready, 1)

                def finish_in(m, position):
                    pool.wait_ge(x1_stored, at(m, 16, 16))
                    pool.sem_inc(x1_free, 1)
                    pool.wait_ge(in_ready, at(m, 2, 2))
                    hold(pool)
                    pool.dma_start(xp_dram[:, bass.ds(position, 1), :].rearrange("k o g -> k (o g)"), xp[:, :]).then_inc(in_stored, 16)

                def output(mm, u, position, x1=x1[:, :]):
                    pool.wait_ge(picked, at(mm, 3, 6))
                    nc.gpsimd.tensor_tensor(base[:, :], x1, h2[:, :], ALU.add).then_inc(part_a, 1)
                    nc.gpsimd.tensor_tensor(w3[:, :], S2[:, u, :], fb[:, 0, :], ALU.mult).then_inc(part_a, 1)
                    pool.wait_ge(part_a, at(mm, 4, 2))
                    nc.gpsimd.tensor_tensor(base[:, :], base[:, :], w3[:, :], ALU.add).then_inc(part_a, 1)
                    pool.wait_ge(part_a, at(mm, 4, 3))
                    nc.gpsimd.tensor_tensor(w3[:, :], S2[:, 1 - u, :], fb[:, 1, :], ALU.mult).then_inc(part_a, 1)
                    pool.wait_ge(part_a, at(mm, 4, 4))
                    nc.gpsimd.tensor_tensor(base[:, :], base[:, :], w3[:, :], ALU.subtract).then_inc(base_ready, 1)
                    pool.wait_ge(base_ready, at(mm, 1, 2))
                    hold(pool)
                    pool.dma_start(base_dram[:, bass.ds(position, 1), :].rearrange("k o d -> k (o d)"), base[:, :]).then_inc(base_stored, 16)
                    pool.wait_ge(base_stored, at(mm, 16, 16))
                    hold(pool)

                def scores(n, p):
                    pool.wait_ge(y_ready, at(n, NP, p + 1))
                    slot = E[:, p % E_SLOTS, :]
                    nc.gpsimd.tensor_tensor(slot, slot, t_row[:, p * PIECE:(p + 1) * PIECE], ALU.add).then_inc(y_sum, 1)

                when = {2: (0, 1), 4: (2,), 7: (3,)}

                def turn(n, u, more, prev):
                    for p in range(NP):
                        q = p + LEAD
                        if q < NP:
                            scores(n, q)
                        elif more:
                            scores(n + 1, q - NP)
                        if prev:
                            m, v = n - 1, 1 - u
                            mm = m - WARM if prev == "main" else None
                            position = m - WARM if prev == "main" else m + OFF
                            for k in when.get(p, ()):
                                if k == 0:
                                    finish_x(m, position)
                                elif k == 1:
                                    finish_rstd(m)
                                elif k == 2:
                                    finish_in(m, position)
                                elif mm is not None:
                                    output(mm, v, position)

                for p in range(LEAD):
                    scores(0, p)
                for _ in tiles(pool, turn):
                    pass
                finish_x(L - 1, OFF - 1)
                finish_rstd(L - 1)
                finish_in(L - 1, OFF - 1)
                output(L - 1 - WARM, 1, OFF - 1)
                with pool.Fori(0, WARM // 2) as i:
                    for u in range(2):
                        output(2 * i + (L - WARM + u), u, 2 * i + (OFF + u), x1_again[u])
                pool.wait_ge(base_stored, 16 * L)
                pool.wait_ge(x1_stored, 16 * L)
                pool.wait_ge(in_stored, 16 * L)

            @block.scalar
            def _(act):
                def scores(n, u, p):
                    if p == 0:
                        act.wait_ge(guard_max, at(n, 6, 6))
                    if not (isinstance(n, int) and n == 0 and p < E_SLOTS):
                        act.wait_ge(turned, at(n, NG, GPP * (p - E_SLOTS + 1)))
                    nc.scalar.activation(E[:, p % E_SLOTS, :], t_row[:, p * PIECE:(p + 1) * PIECE], ACT.Relu,
                                         bias=BIAS1[u], scale=1.0 / SLOPE - 1.0).then_inc(y_ready, 1)

                def exponentials(n, u, p):
                    act.wait_ge(y_sum, at(n, NP, p + 1))
                    slot = E[:, p % E_SLOTS, :]
                    nc.scalar.activation(slot, slot, ACT.Exp, bias=BIAS2[u], scale=SLOPE).then_inc(e_ready, 1)

                def collect(n, g):
                    act.wait_ge(turned, at(n, NG, g + 1))
                    nc.scalar.copy(PT[:, g % 2, :], ps_t[g % 2][:, :]).then_inc(pt_ready, 1)

                def gates(m, xp=xp[:, :]):
                    act.wait_ge(gate_sum, at(m, 2, 4))
                    nc.scalar.activation(xp, xp, ACT.Tanh).then_inc(gate_act, 1)

                def cell_out(m):
                    act.wait_ge(cell, at(m, 3, 3))
                    nc.scalar.activation(w1[:, :], c2[:, :], ACT.Tanh, scale=0.5).then_inc(cell_act, 1)

                def state_turned(m):
                    act.wait_ge(hT_mm, at(m, 1, 1))
                    nc.scalar.copy(hT[:, :, :].rearrange("p k q -> p (k q)"), ps_h[:, 0:D]).then_inc(hT_ready, 1)

                when = {4: 0, 6: 1, 11: 2, 12: 3, 13: 4}

                def turn(n, u, more, prev):
                    for g in range(NG):
                        if g % GPP == 0:
                            for part, lead in ((exponentials, LEAD), (scores, LEAD + 1)):
                                p = g // GPP + lead
                                if p < NP:
                                    part(n, u, p)
                                elif more:
                                    part(n + 1, 1 - u, p - NP)
                        collect(n, g)
                        if prev:
                            for h, k in when.items():
                                if h == g:
                                    m, v = n - 1, 1 - u
                                    if k == 0:
                                        act.wait_ge(fin, at(m, FIN, 7))
                                        nc.scalar.activation(w2[:, :], w2[:, :], ACT.Tanh, scale=0.5).then_inc(elu_ready, 1)
                                    elif k == 1:
                                        act.wait_ge(xnT_mm, at(m, 1, 1))
                                        nc.scalar.copy(xnT[:, :, :].rearrange("p k q -> p (k q)"), ps_x[:, 0:D]).then_inc(xnT_ready, 1)
                                    elif k == 2:
                                        gates(m)
                                    elif k == 3:
                                        cell_out(m)
                                    else:
                                        state_turned(m)

                scores(0, 0, 0)
                for p in range(LEAD):
                    exponentials(0, 0, p)
                    scores(0, 0, p + 1)
                for _ in tiles(act, turn):
                    act.wait_ge(h_ready, WARM)
                    act.dma_start(end_dram[0], h2[:, :]).then_inc(end_stored, 16)
                    act.dma_start(end_dram[1], c2[:, :]).then_inc(end_stored, 16)
                    act.wait_ge(shift_mm, 1)
                    nc.scalar.copy(hT[:, :, :].rearrange("p k q -> p (k q)"), ps_h[:, 0:D]).then_inc(shifted_h, 1)
                m = L - 1
                act.wait_ge(fin, at(m, FIN, 7))
                nc.scalar.activation(w2[:, :], w2[:, :], ACT.Tanh, scale=0.5).then_inc(elu_ready, 1)
                act.wait_ge(xnT_mm, m + 1)
                nc.scalar.copy(xnT[:, :, :].rearrange("p k q -> p (k q)"), ps_x[:, 0:D]).then_inc(xnT_ready, 1)

                def step(m, xp=xp[:, :]):
                    gates(m, xp)
                    cell_out(m)
                    state_turned(m)
                step(L - 1)
                with act.Fori(0, WARM // 2) as i:
                    for u in range(2):
                        step(2 * i + (L + u), xp_again[u])

            @block.vector
            def _(dve):
                def guard(n, u, c):
                    dve.wait_ge(adj_loaded[c % 2], at(n, 16 * NCH // 2, 16 * (c // 2) + 16))
                    hold(dve)
                    nc.vector.tensor_tensor_reduce(out=nb[:, u, c * CHUNK:(c + 1) * CHUNK], in0=adj_sb[:, c % 2, :],
                                                   in1=t_row[:, c * CHUNK:(c + 1) * CHUNK], scale=1.0, scalar=0.0,
                                                   op0=ALU.mult, op1=ALU.max, accum_out=gmx[:, u, c:c + 1]).then_inc(guard_done, 1)

                def row_max(n, u):
                    dve.wait_ge(guard_done, at(n, NCH, NCH))
                    nc.vector.tensor_reduce(out=GM[u], in_=gmx[:, u, :], axis=AX.X, op=ALU.max).then_inc(guard_max, 1)
                    nc.vector.tensor_copy(SC, s_perm[:, bass.ds(n, 1)]).then_inc(guard_max, 1)
                    dve.wait_ge(guard_max, at(n, 6, 2))
                    nc.vector.tensor_tensor(Z1, GM[u], SC, ALU.add).then_inc(guard_max, 1)
                    dve.wait_ge(guard_max, at(n, 6, 3))
                    nc.vector.tensor_scalar(Z2, Z1, -SLOPE, -1.0, ALU.mult, ALU.add)
                    nc.vector.tensor_scalar(Z3, Z1, -1.0, -1.0, ALU.mult, ALU.add).then_inc(guard_max, 1)
                    dve.wait_ge(guard_max, at(n, 6, 4))
                    nc.vector.tensor_tensor(NEGM, Z2, Z3, ALU.min).then_inc(guard_max, 1)
                    dve.wait_ge(guard_max, at(n, 6, 5))
                    nc.vector.tensor_scalar(BIAS1[u], SC, 1.0 / SLOPE - 1.0, None, ALU.mult)
                    nc.vector.scalar_tensor_tensor(out=BIAS2[u], in0=SC, scalar=SLOPE, in1=NEGM, op0=ALU.mult,
                                                   op1=ALU.add).then_inc(guard_max, 1)

                def weights(n, u, p):
                    e = E[:, p % E_SLOTS, :]
                    dve.wait_ge(e_ready, at(n, NP, p + 1))
                    nc.vector.scalar_tensor_tensor(out=e, in0=nb[:, u, p * PIECE:(p + 1) * PIECE], scalar=0.0, in1=e,
                                                   op0=ALU.is_gt, op1=ALU.min, accum_out=rs[:, u, p:p + 1]).then_inc(p_ready, 1)

                def counted(m, first):
                    k = [first]

                    def step(ins, wait=True):
                        k[0] += 1
                        ins.then_inc(fin, 1)
                        if wait:
                            dve.wait_ge(fin, at(m, FIN, k[0]))
                    return step

                def divide(m, u):
                    step, v = counted(m, 0), nc.vector
                    dve.wait_ge(p_ready, at(m, NP, NP))
                    step(v.tensor_reduce(out=RSUM, in_=rs[:, u, :], axis=AX.X, op=ALU.add), False)
                    step(v.tensor_scalar(NONE, GM[u], 0.0, None, ALU.is_le))
                    step(v.scalar_tensor_tensor(out=DEN, in0=NONE, scalar=float(N), in1=RSUM, op0=ALU.mult, op1=ALU.add))
                    step(v.reciprocal(RINV, DEN), False)
                    dve.wait_ge(acc_ready, at(m, 1, 1))
                    step(v.scalar_tensor_tensor(out=w1b[:, :], in0=csum[:, :], scalar=NONE, in1=ps_o[u][:, 0:D], op0=ALU.mult, op1=ALU.add))
                    step(v.tensor_scalar(w1b[:, :], w1b[:, :], RINV, None, ALU.mult))
                    step(v.tensor_scalar(w2[:, :], w1b[:, :], 0.0, None, ALU.min), False)
                    dve.wait_ge(xi_loaded[u], at(m, 8, 16 - 8 * u))
                    step(v.scalar_tensor_tensor(out=w1b[:, :], in0=w1b[:, :], scalar=0.0, in1=x_in[:, u, :], op0=ALU.max, op1=ALU.add), False)

                def normalise(m, mm):
                    step, v = counted(m, 8), nc.vector
                    dve.wait_ge(elu_ready, at(m, 1, 1))
                    step(v.tensor_scalar(xn[:, :], w2[:, :], -1.0, 1.0, ALU.mult, ALU.add))
                    step(v.reciprocal(xn[:, :], xn[:, :]))
                    step(v.scalar_tensor_tensor(out=w2[:, :], in0=w2[:, :], scalar=2.0, in1=xn[:, :], op0=ALU.mult, op1=ALU.mult))
                    dve.wait_ge(x1_free, at(m, 1, 1))
                    if mm is not None:
                        dve.wait_ge(base_ready, at(mm, 1, 1))
                    step(v.tensor_tensor(x1[:, :], w1b[:, :], w2[:, :], ALU.add))
                    step(v.bn_stats(STATS, x1[:, :]))
                    hold(dve)
                    step(v.bn_aggr(MV, STATS))
                    step(v.tensor_scalar(VE, MV[:, 1:2], EPS, None, ALU.add), False)
                    dve.wait_ge(rstd_ready, at(m, 1, 1))
                    step(v.tensor_scalar(xn[:, :], x1[:, :], MV[:, 0:1], RSTD, ALU.subtract, ALU.mult), False)

                def inputs(m):
                    for h in range(2):
                        dve.wait_ge(in_mm, at(m, 2, h + 1))
                        nc.vector.tensor_tensor(xp[:, h * HALF:(h + 1) * HALF], ps_g[h][:, :], bias[:, h * HALF:(h + 1) * HALF],
                                                ALU.add).then_inc(in_ready, 1)

                def gates(m, xp=xp, stored=True):
                    if stored:
                        dve.wait_ge(in_stored, at(m, 16, 16))
                    for h in range(2):
                        dve.wait_ge(rec_mm, at(m, 2, h + 1))
                        half = xp[:, h * HALF:(h + 1) * HALF]
                        nc.vector.tensor_tensor(half, half, ps_g[h][:, :], ALU.add).then_inc(gate_sum, 1)

                def new_cell(m, xp=xp):
                    dve.wait_ge(gate_act, at(m, 1, 1))
                    nc.vector.scalar_tensor_tensor(out=w1b[:, :], in0=xp[:, D:2 * D], scalar=1.0, in1=c2[:, :],
                                                   op0=ALU.add, op1=ALU.mult).then_inc(cell, 1)
                    nc.vector.scalar_tensor_tensor(out=xn[:, :], in0=xp[:, 0:D], scalar=1.0, in1=xp[:, 2 * D:3 * D],
                                                   op0=ALU.add, op1=ALU.mult).then_inc(cell, 1)
                    dve.wait_ge(cell, at(m, 3, 2))
                    nc.vector.scalar_tensor_tensor(out=c2[:, :], in0=w1b[:, :], scalar=0.5, in1=xn[:, :],
                                                   op0=ALU.mult, op1=ALU.add).then_inc(cell, 1)

                def new_state(m, mm, xp=xp):
                    if mm is not None:
                        dve.wait_ge(base_ready, at(mm, 1, 1))
                    dve.wait_ge(cell_act, at(m, 1, 1))
                    nc.vector.scalar_tensor_tensor(out=h2[:, :], in0=xp[:, 3 * D:G4], scalar=1.0, in1=w1[:, :],
                                                   op0=ALU.add, op1=ALU.mult).then_inc(h_ready, 1)

                def pick(m, mm, u):
                    dve.wait_ge(logit_mm, at(mm, 1, 1))
                    nc.vector.tensor_scalar(LD, ps_h[:, 0:1], BL[:, 0:1], None, ALU.add).then_inc(picked, 1)
                    dve.wait_ge(picked, at(mm, 3, 4))
                    nc.vector.tensor_scalar(LG, ps_h[:, 1:2], BL[:, 1:2], LD, ALU.add, ALU.is_gt).then_inc(picked, 1)
                    dve.wait_ge(picked, at(mm, 3, 5))
                    nc.vector.scalar_tensor_tensor(out=S2[:, 1 - u, :], in0=h2[:, :], scalar=LG, in1=S2[:, u, :],
                                                   op0=ALU.mult, op1=ALU.add).then_inc(picked, 1)

                when = {1: 0, 2: 1, 4: 2, 5: 3, 6: 4, 7: 5}

                def turn(n, u, more, prev):
                    for p in range(NP):
                        weights(n, u, p)
                        if prev:
                            m, v = n - 1, 1 - u
                            mm = m - WARM if prev == "main" else None
                            for h, k in when.items():
                                if h == p:
                                    if k == 0:
                                        divide(m, v)
                                    elif k == 1:
                                        normalise(m, mm)
                                    elif k == 2:
                                        inputs(m)
                                    elif k == 3:
                                        gates(m)
                                    elif k == 4:
                                        new_cell(m)
                                        new_state(m, mm)
                                    elif mm is not None:
                                        pick(m, mm, v)
                        if more and p < NCH:
                            guard(n + 1, 1 - u, p)
                        if more and p == NCH:
                            row_max(n + 1, 1 - u)

                for c in range(NCH):
                    guard(0, 0, c)
                row_max(0, 0)
                for _ in tiles(dve, turn):
                    dve.wait_ge(end_stored, 32)
                    dve.wait_ge(shift_mm, 1)
                    nc.vector.tensor_copy(c2[:, :], ps_x[:, D:2 * D]).then_inc(shifted, 1)
                divide(L - 1, 1)
                normalise(L - 1, L - 1 - WARM)
                inputs(L - 1)
                gates(L - 1)
                new_cell(L - 1)
                new_state(L - 1, L - 1 - WARM)
                pick(L - 1, L - 1 - WARM, 1)
                with dve.Fori(0, WARM // 2) as i:
                    for u in range(2):
                        m, mm = 2 * i + (L + u), 2 * i + (L - WARM + u)
                        dve.wait_ge(again_in[u], 32 * i + 32)
                        gates(m, xp_again[u], False)
                        new_cell(m, xp_again[u])
                        new_state(m, mm, xp_again[u])
                        pick(m, mm, u)

            @block.tensor
            def _(pe):
                def turned_group(n, g):
                    if g % GPP == 0:
                        pe.wait_ge(p_ready, at(n, NP, g // GPP + 1))
                    p, first = g // GPP, g % GPP * GROUP
                    for b in range(BPG):
                        last = nc.tensor.transpose(ps_t[g % 2][:, b * P:(b + 1) * P],
                                                   E[:, p % E_SLOTS, first + b * P:first + (b + 1) * P], ident[:, :])
                    last.then_inc(turned, 1)

                def summed_group(n, u, g):
                    pe.wait_ge(pt_ready, at(n, NG, g + 1))
                    for b in range(BPG):
                        last = nc.tensor.matmul(ps_o[u][:, 0:D], PT[:, g % 2, b * P:(b + 1) * P], wh[:, g * BPG + b, :],
                                                start=g == 0 and b == 0, stop=g == NG - 1 and b == BPG - 1)
                    if g == NG - 1:
                        last.then_inc(acc_ready, 1)

                def x_turned(m):
                    pe.wait_ge(fin, at(m, FIN, 16))
                    for k in range(KD):
                        last = nc.tensor.transpose(ps_x[:, k * P:(k + 1) * P], xn[:, k * P:(k + 1) * P], ident[:, :])
                    last.then_inc(xnT_mm, 1)

                def x_product(m):
                    pe.wait_ge(xnT_ready, at(m, 1, 1))
                    pe.wait_ge(gate_sum, at(m, 2, 2))
                    for h in range(2):
                        for k in range(KD):
                            last = nc.tensor.matmul(ps_g[h][:, :], xnT[:, k, :], wih[:, k, h * HALF:(h + 1) * HALF], start=k == 0, stop=k == KD - 1)
                        last.then_inc(in_mm, 1)

                def h_product(m, fresh=True):
                    if fresh:
                        pe.wait_ge(in_ready, at(m, 2, 2))
                    else:
                        pe.wait_ge(gate_sum, at(m, 2, 2))
                    pe.wait_ge(hT_ready, at(m, 1, 1))
                    for h in range(2):
                        for k in range(KD):
                            last = nc.tensor.matmul(ps_g[h][:, :], hT[:, k, :], whh[:, k, h * HALF:(h + 1) * HALF], start=k == 0, stop=k == KD - 1)
                        last.then_inc(rec_mm, 1)

                def h_turned(m, mm):
                    pe.wait_ge(h_ready, at(m, 1, 1))
                    if mm is not None:
                        pe.wait_ge(picked, at(mm, 3, 3))
                    for k in range(KD):
                        last = nc.tensor.transpose(ps_h[:, k * P:(k + 1) * P], h2[:, k * P:(k + 1) * P], ident[:, :])
                    last.then_inc(hT_mm, 1)

                def logits(m, mm):
                    pe.wait_ge(hT_ready, at(m, 1, 2))
                    for k in range(KD):
                        last = nc.tensor.matmul(ps_h[:, 0:2], hT[:, k, :], wl[:, k, :], start=k == 0, stop=k == KD - 1)
                    last.then_inc(logit_mm, 1)

                when = {6: (0,), 7: (1,), 9: (2,), 13: (3,), 14: (4,)}

                def turn(n, u, more, prev):
                    for g in range(NG):
                        turned_group(n, g)
                        if g > 0:
                            summed_group(n, u, g - 1)
                        elif prev:
                            summed_group(n - 1, 1 - u, NG - 1)
                        if prev:
                            m, v = n - 1, 1 - u
                            mm = m - WARM if prev == "main" else None
                            for k in when.get(g, ()):
                                if k == 0:
                                    x_turned(m)
                                elif k == 1:
                                    x_product(m)
                                elif k == 2:
                                    h_product(m)
                                elif k == 3:
                                    h_turned(m, mm)
                                elif mm is not None:
                                    logits(m, mm)

                for _ in tiles(pe, turn):
                    pe.wait_ge(shift_made, 2)
                    pe.wait_ge(h_ready, WARM)
                    pe.wait_ge(hT_ready, WARM + 1)
                    for k in range(KD):
                        nc.tensor.matmul(ps_h[:, k * P:(k + 1) * P], h2[:, k * P:(k + 1) * P], shift[:, :], start=True, stop=True)
                    nc.tensor.matmul(ps_x[:, D:2 * D], shift[:, :], c2[:, :], start=True, stop=True).then_inc(shift_mm, 1)
                    pe.wait_ge(shifted, 1)
                    pe.wait_ge(shifted_h, 1)
                summed_group(L - 1, 1, NG - 1)
                x_turned(L - 1)
                x_product(L - 1)
                h_product(L - 1)
                h_turned(L - 1, L - 1 - WARM)
                logits(L - 1, L - 1 - WARM)
                with pe.Fori(0, WARM // 2) as i:
                    for u in range(2):
                        m, mm = 2 * i + (L + u), 2 * i + (L - WARM + u)
                        h_product(m, False)
                        h_turned(m, mm)
                        logits(m, mm)

        end_in, differ, differ_max, decided = sem("end_in"), sem("differ"), sem("differ_max"), sem("decided")
        with nc.Block() as block:
            @block.sync
            def _(sp):
                sp.dma_start(x_in[:, 0, :], end_dram[0]).then_inc(end_in, 16)
                sp.dma_start(x_in[:, 1, :], end_dram[1]).then_inc(end_in, 16)

            @block.vector
            def _(dve):
                v = nc.vector
                dve.wait_ge(end_in, 32)
                v.tensor_tensor(x_in[:, 0, :], x_in[:, 0, :], h2[:, :], ALU.subtract)
                v.tensor_tensor(x_in[:, 1, :], x_in[:, 1, :], c2[:, :], ALU.subtract).then_inc(differ, 1)
                dve.wait_ge(differ, 1)
                v.tensor_reduce(out=DMX[:, 0:1], in_=x_in[:, :, :], axis=AX.XY, op=ALU.max,
                                apply_absolute_value=True).then_inc(differ, 1)
                dve.wait_ge(differ_max, 1)
                v.tensor_reduce(out=DMX[0:1, 1:2], in_=ps_x[0:1, 0:P], axis=AX.X, op=ALU.max).then_inc(differ, 1)
                dve.wait_ge(differ, 3)
                v.tensor_scalar(DMX[0:1, 2:3], DMX[0:1, 1:2], TOL, None, ALU.is_le).then_inc(differ, 1)
                dve.wait_ge(differ, 4)
                v.tensor_scalar(flag[0:1, 0:1], DMX[0:1, 2:3], -1.0, 1.0, ALU.mult, ALU.add).then_inc(decided, 1)

            @block.tensor
            def _(pe):
                pe.wait_ge(differ, 2)
                nc.tensor.matmul(ps_x[0:1, 0:P], DMX[:, 0:1], ident[:, :], start=True, stop=True).then_inc(differ_max, 1)

        g_load, g_store = sem("g_load"), sem("g_store")
        g_in, g_step, g_shift = sem("g_in"), sem("g_step"), sem("g_shift")
        g_start_h, g_start_c = sem("g_start_h"), sem("g_start_c")
        g_rec, g_sum, g_act, g_cell, g_cell_act = sem("g_rec"), sem("g_sum"), sem("g_act"), sem("g_cell"), sem("g_cell_act")
        g_h, g_hT_mm, g_hT, g_logit, g_base = sem("g_h"), sem("g_hT_mm"), sem("g_hT"), sem("g_logit"), sem("g_base")

        def sweeps(eng, start, step):
            needed = eng.value_load(flag[0:1, 0:1], min_val=0, max_val=1)
            with eng.If(needed):
                with eng.Fori(0, SWEEPS) as q:
                    start(q)
                    with eng.Fori(0, L) as l:
                        step(q * L + l, l)

        with nc.Block() as block:
            @block.sync
            def _(sp):
                def step(r, l):
                    sp.wait_ge(g_step, r + 1)
                    hold(sp)
                    sp.dma_start(xp_again[0], xp_dram[:, bass.ds(l, 1), :].rearrange("k o g -> k (o g)")).then_inc(g_load, 16)
                    sp.dma_start(x1_again[0], x1_dram[:, bass.ds(l, 1), :].rearrange("k o d -> k (o d)")).then_inc(g_load, 16)
                    sp.wait_ge(g_load, 32)
                    sp.sem_clear(g_load)
                    sp.sem_inc(g_in, 1)
                    sp.wait_ge(g_base, r + 1)
                    hold(sp)
                    sp.dma_start(base_dram[:, bass.ds(l, 1), :].rearrange("k o d -> k (o d)"), base[:, :]).then_inc(g_store, 16)
                    sp.wait_ge(g_store, 16)
                    sp.sem_clear(g_store)
                    sp.sem_inc(g_step, 1)
                sp.sem_inc(g_step, 1)
                sweeps(sp, lambda q: None, step)

            @block.tensor
            def _(pe):
                def start(q):
                    pe.wait_ge(g_step, q * L + 1)
                    for k in range(KD):
                        nc.tensor.matmul(ps_h[:, k * P:(k + 1) * P], h2[:, k * P:(k + 1) * P], shift[:, :], start=True, stop=True)
                    nc.tensor.matmul(ps_x[:, D:2 * D], shift[:, :], c2[:, :], start=True, stop=True).then_inc(g_shift, 1)
                    pe.wait_ge(g_start_h, q + 1)
                    hold(pe)

                def step(r, l):
                    pe.wait_ge(g_step, r + 1)
                    for h in range(2):
                        for k in range(KD):
                            last = nc.tensor.matmul(ps_g[h][:, :], hT[:, k, :], whh[:, k, h * HALF:(h + 1) * HALF], start=k == 0, stop=k == KD - 1)
                    last.then_inc(g_rec, 1)
                    pe.wait_ge(g_h, r + 1)
                    for k in range(KD):
                        last = nc.tensor.transpose(ps_h[:, k * P:(k + 1) * P], h2[:, k * P:(k + 1) * P], ident[:, :])
                    last.then_inc(g_hT_mm, 1)
                    pe.wait_ge(g_hT, r + 1)
                    for k in range(KD):
                        last = nc.tensor.matmul(ps_h[:, 0:2], hT[:, k, :], wl[:, k, :], start=k == 0, stop=k == KD - 1)
                    last.then_inc(g_logit, 1)
                sweeps(pe, start, step)

            @block.scalar
            def _(act):
                def start(q):
                    act.wait_ge(g_shift, q + 1)
                    nc.scalar.copy(hT[:, :, :].rearrange("p k q -> p (k q)"), ps_h[:, 0:D]).then_inc(g_start_h, 1)

                def step(r, l):
                    act.wait_ge(g_sum, r + 1)
                    nc.scalar.activation(xp_again[0], xp_again[0], ACT.Tanh).then_inc(g_act, 1)
                    act.wait_ge(g_cell, r + 1)
                    nc.scalar.activation(w1[:, :], c2[:, :], ACT.Tanh, scale=0.5).then_inc(g_cell_act, 1)
                    act.wait_ge(g_hT_mm, r + 1)
                    nc.scalar.copy(hT[:, :, :].rearrange("p k q -> p (k q)"), ps_h[:, 0:D]).then_inc(g_hT, 1)
                sweeps(act, start, step)

            @block.vector
            def _(dve):
                v = nc.vector
                g = xp_again[0]
                S = S2[:, 0, :]

                def start(q):
                    dve.wait_ge(g_shift, q + 1)
                    v.tensor_copy(c2[:, :], ps_x[:, D:2 * D])
                    v.memset(S, 0.0)
                    dve.drain()

                def step(r, l):
                    dve.wait_ge(g_in, r + 1)
                    hold(dve)
                    dve.wait_ge(g_rec, r + 1)
                    for h in range(2):
                        half = g[:, h * HALF:(h + 1) * HALF]
                        last = v.tensor_tensor(half, half, ps_g[h][:, :], ALU.add)
                    last.then_inc(g_sum, 1)
                    dve.wait_ge(g_act, r + 1)
                    v.scalar_tensor_tensor(out=w1b[:, :], in0=g[:, D:2 * D], scalar=1.0, in1=c2[:, :], op0=ALU.add, op1=ALU.mult)
                    v.scalar_tensor_tensor(out=xn[:, :], in0=g[:, 0:D], scalar=1.0, in1=g[:, 2 * D:3 * D], op0=ALU.add, op1=ALU.mult)
                    dve.drain()
                    v.scalar_tensor_tensor(out=c2[:, :], in0=w1b[:, :], scalar=0.5, in1=xn[:, :], op0=ALU.mult, op1=ALU.add).then_inc(g_cell, 1)
                    dve.wait_ge(g_cell_act, r + 1)
                    v.scalar_tensor_tensor(out=h2[:, :], in0=g[:, 3 * D:G4], scalar=1.0, in1=w1[:, :], op0=ALU.add, op1=ALU.mult).then_inc(g_h, 1)
                    dve.wait_ge(g_logit, r + 1)
                    v.tensor_scalar(LD, ps_h[:, 0:1], BL[:, 0:1], None, ALU.add)
                    v.tensor_tensor(base[:, :], x1_again[0], h2[:, :], ALU.add)
                    v.tensor_tensor(w2[:, :], S, fb[:, 0, :], ALU.mult)
                    dve.drain()
                    v.tensor_scalar(LG, ps_h[:, 1:2], BL[:, 1:2], LD, ALU.add, ALU.is_gt)
                    v.tensor_tensor(base[:, :], base[:, :], w2[:, :], ALU.add)
                    dve.drain()
                    v.scalar_tensor_tensor(out=S, in0=h2[:, :], scalar=LG, in1=S, op0=ALU.mult, op1=ALU.add)
                    dve.drain()
                    v.tensor_tensor(w2[:, :], S, fb[:, 1, :], ALU.mult)
                    dve.drain()
                    v.tensor_tensor(base[:, :], base[:, :], w2[:, :], ALU.subtract).then_inc(g_base, 1)
                sweeps(dve, start, step)

        tot_mm, off_ready, add_ready, base_in = sem("tot_mm"), sem("off_ready"), sem("add_ready"), sem("base_in")
        out_ready, out_stored, tables = sem("out_ready"), sem("out_stored"), sem("tables")
        OB = 8
        OW = L // OB
        with nc.Block() as block:
            @block.gpsimd
            def _(pool):
                nc.gpsimd.memset(strict, 1.0).then_inc(tables, 1)
                nc.gpsimd.memset(ones, 1.0).then_inc(tables, 1)
                pool.wait_ge(tables, 2)
                nc.gpsimd.affine_select(out=strict, in_=strict, compare_op=ALU.is_gt, fill=0.0,
                                        base=0, pattern=[[1, P]], channel_multiplier=-1).then_inc(tables, 1)

            @block.tensor
            def _(pe):
                pe.wait_ge(tables, 3)
                nc.tensor.matmul(ps_x[:, 0:D], strict, S2[:, 0, :], start=True, stop=True)
                nc.tensor.matmul(ps_h[:, 0:D], ones, S2[:, 0, :], start=True, stop=True).then_inc(tot_mm, 1)

            @block.sync
            def _(sp):
                for i in range(OB):
                    sp.dma_start(wh[:, i * OW:(i + 1) * OW, :], base_dram[:, i * OW:(i + 1) * OW, :]).then_inc(base_in, 16)
                for i in range(OB):
                    sp.wait_ge(out_ready, i + 1)
                    sp.dma_start(out_kl[:, i * OW:(i + 1) * OW, :], wh[:, i * OW:(i + 1) * OW, :]).then_inc(out_stored, 16)
                sp.wait_ge(out_stored, 16 * OB)

            @block.vector
            def _(dve):
                v = nc.vector
                dve.wait_ge(tot_mm, 1)
                v.tensor_copy(w1[:, :], ps_x[:, 0:D]).then_inc(off_ready, 1)
                dve.wait_ge(off_ready, 1)
                v.tensor_tensor(w2[:, :], ps_h[:, 0:D], w1[:, :], ALU.subtract).then_inc(off_ready, 1)
                v.tensor_tensor(w1[:, :], w1[:, :], fb[:, 0, :], ALU.mult).then_inc(off_ready, 1)
                dve.wait_ge(off_ready, 2)
                v.tensor_tensor(w2[:, :], w2[:, :], fb[:, 1, :], ALU.mult).then_inc(off_ready, 1)
                dve.wait_ge(off_ready, 4)
                v.tensor_tensor(w1[:, :], w1[:, :], w2[:, :], ALU.add).then_inc(off_ready, 1)
                dve.wait_ge(off_ready, 5)
                for i in range(OB):
                    dve.wait_ge(base_in, 16 * OB)
                    part = wh[:, i * OW:(i + 1) * OW, :]
                    v.tensor_tensor(part, part, w1[:, :].rearrange("p (o d) -> p o d", o=1).to_broadcast([P, OW, D]),
                                    ALU.add).then_inc(out_ready, 1)


def kernel(x, adj, L0_gnn_W, L0_gnn_a, L0_ffn_W_ih, L0_ffn_W_hh, L0_ffn_b_ih, L0_ffn_b_hh, L0_ffn_W_lin,
           L0_ffn_b_lin, L0_ffn_fw_att, L0_ffn_bw_att):
    import numpy as np
    import concourse.bacc as bacc
    from concourse import mybir as mb
    from concourse.bass_utils import run_bass_kernel_spmd as run

    nc = bacc.Bacc("TRN2", target_bir_lowering=False, num_devices=1)
    laid = [("x", x), ("adj", adj), ("w_gnn", L0_gnn_W), ("a_pair", L0_gnn_a), ("w_ih_t", np.asarray(L0_ffn_W_ih).T),
            ("w_hh_t", np.asarray(L0_ffn_W_hh).T), ("b_ih", L0_ffn_b_ih), ("b_hh", L0_ffn_b_hh),
            ("w_lin_t", np.asarray(L0_ffn_W_lin).T), ("b_lin", L0_ffn_b_lin), ("fw", L0_ffn_fw_att), ("bw", L0_ffn_bw_att)]
    arrays, args = {}, []
    for name, a in laid:
        a = np.ascontiguousarray(a)
        arrays[name] = a
        args.append(nc.dram_tensor(name, a.shape, mb.dt.from_np(a.dtype), kind="ExternalInput").ap())
    args.append(nc.dram_tensor("out", x.shape, mb.dt.float32, kind="ExternalOutput").ap())
    adj_ffn_kernel(nc, *args)
    return run(nc, [arrays], core_ids=[0]).results[0]["out"]
```

```python
from contextlib import ExitStack

import concourse.bass as bass
from concourse import mybir

F32 = mybir.dt.float32
BF16 = mybir.dt.bfloat16
I32 = mybir.dt.int32
ALU = mybir.AluOpType
ACT = mybir.ActivationFunctionType
AX = mybir.AxisListType

P = 128
D = 256
KD = D // P
G4 = 4 * D
HALF = G4 // 2
EPS = 1e-5
SLOPE = 0.2
TOL = 2.0 ** -19
CHUNK = 2048
PIECE = 1024
GROUP = 512
E_SLOTS = 4


def adj_ffn_kernel(nc, x, adj, w_gnn, a_pair, w_ih_t, w_hh_t, b_ih, b_hh, w_lin_t, b_lin, fw, bw, out, warm=32, SWEEPS=P - 1):
    N = x.shape[0]
    L = N // P
    NCH, NP, NG = N // CHUNK, N // PIECE, N // GROUP
    BPG = GROUP // P
    GPP = PIECE // GROUP
    WARM = warm
    OFF = L - WARM

    x_kl = x.rearrange("(k l) d -> k l d", l=L)
    adj_kl = adj.rearrange("(k l) j -> k l j", l=L)
    out_kl = out.rearrange("(k l) d -> k l d", l=L)
    t_line = nc.dram_tensor("t_line", [N], F32, kind="Internal").ap()
    s_line = nc.dram_tensor("s_line", [N], F32, kind="Internal").ap()
    xp_dram = nc.dram_tensor("xp_dram", [P, L, G4], F32, kind="Internal").ap()
    x1_dram = nc.dram_tensor("x1_dram", [P, L, D], F32, kind="Internal").ap()
    end_dram = nc.dram_tensor("end_dram", [2, P, D], F32, kind="Internal").ap()
    base_dram = nc.dram_tensor("base_dram", [P, L, D], F32, kind="Internal").ap()

    with ExitStack() as ctx:
        def sb(name, shape, dt=F32):
            return ctx.enter_context(nc.sbuf_tensor(name, shape, dt))

        def pb(name):
            return ctx.enter_context(nc.psum_tensor(name, [P, 512], F32))

        def sem(name):
            return ctx.enter_context(nc.semaphore(name))

        def hold(eng):
            eng.sem_inc(held, 1)

        wh = sb("wh", [P, L, D])
        t_row = sb("t_row", [P, N])
        adj_sb = sb("adj_sb", [P, 2, CHUNK])
        nb = sb("nb", [P, 2, N], BF16)
        E = sb("E", [P, E_SLOTS, PIECE])
        PT = sb("PT", [P, 2, GROUP])
        wih = sb("wih", [P, KD, G4])
        whh = sb("whh", [P, KD, G4])
        bias = sb("bias", [P, G4])
        xp = sb("xp", [P, G4])
        ident = sb("ident", [P, P])
        shift = sb("shift", [P, P])
        w1b = sb("w1b", [P, D])
        w3 = sb("w3", [P, D])
        small = sb("small", [P, 64])
        x_in = sb("x_in", [P, 2, D])
        x1 = sb("x1", [P, D])
        w1 = sb("w1", [P, D])
        w2 = sb("w2", [P, D])
        xn = sb("xn", [P, D])
        xnT = sb("xnT", [P, KD, P])
        hT = sb("hT", [P, KD, P])
        c2 = sb("c2", [P, D])
        h2 = sb("h2", [P, D])
        csum = sb("csum", [P, D])
        S2 = sb("S2", [P, 2, D])
        fb = sb("fb", [P, 2, D])
        base = sb("base", [P, D])
        s_perm = sb("s_perm", [P, L])
        wl = sb("wl", [P, KD, 2])
        rs = sb("rs", [P, 2, NP])
        gmx = sb("gmx", [P, 2, NCH])
        flag = sb("flag", [P, 2], I32)

        ps_t = [pb("ps_t0"), pb("ps_t1")]
        ps_o = [pb("ps_o0"), pb("ps_o1")]
        ps_x, ps_h = pb("ps_x"), pb("ps_h")
        ps_g = [pb("ps_g0"), pb("ps_g1")]

        def col(k, n=1):
            return small[:, k:k + n]
        BL, TMIN, MHALF = col(0, 2), col(2), col(3)
        BIAS1 = [col(4), col(5)]
        BIAS2 = [col(6), col(7)]
        GM = [col(8), col(9)]
        Z1, Z2, Z3, SC, NEGM = col(10), col(11), col(12), col(34), col(35)
        RSUM, NONE, DEN, RINV = col(13), col(14), col(15), col(16)
        STATS, MV, VE, RSTD = col(17, 6), col(23, 2), col(25), col(26)
        LD, LG = col(27), col(28)
        PAD = col(29)
        DMX = col(30, 4)

        x_all = wh
        strict = E[:, 0, 0:P]
        WX = D + 2
        w_sb = E[:, 1, 0:KD * WX].rearrange("p (k d) -> p k d", k=KD)
        a_row = E[:, 2, 0:2 * D].rearrange("p (k d) -> p k d", k=2)
        ones = E[:, 3, 0:P]
        stat_all = nb[:, 0, 0:16 * L].bitcast(F32)
        mv_all = nb[:, 0, 16 * L:20 * L].bitcast(F32)
        rstd_all = nb[:, 0, 20 * L:22 * L].bitcast(F32)
        half_all = nb[:, 0, 22 * L:24 * L].bitcast(F32)
        hn = adj_sb[:, :, 0:D]
        hnT = adj_sb[:, :, D:2 * D].rearrange("p u (k q) -> p u k q", k=KD)
        dump = adj_sb[:, :, 2 * D:3 * D]
        part_sum = adj_sb[:, 0, 3 * D:4 * D]
        xp_again = [nb[:, u, 0:2 * G4].bitcast(F32) for u in range(2)]
        x1_again = [nb[:, u, 2 * G4:2 * G4 + 2 * D].bitcast(F32) for u in range(2)]
        st_cols = base[:, 0:2 * L].rearrange("p (a b) -> p a b", a=2)
        st_out = w1[:, :].rearrange("p (a b) -> p a b", a=2)

        XL = 8
        XB = L // XL
        x_loaded = [sem(f"x_loaded{i}") for i in range(XL)]
        w_loaded, row_loaded = sem("w_loaded"), sem("row_loaded")
        consts = sem("consts")
        st_done, ag_done = sem("st_done"), sem("ag_done")
        rs_done, rs_in = sem("rs_done"), sem("rs_in")
        hn_ready, hnT_mm, hnT_ready = sem("hn_ready"), sem("hnT_mm"), sem("hnT_ready")
        wh_mm, wh_ready, st_ready = sem("wh_mm"), sem("wh_ready"), sem("st_ready")
        cs_mm, stT_mm, stT_ready = sem("cs_mm"), sem("stT_mm"), sem("stT_ready")
        line_stored, line_loaded = sem("line_stored"), sem("line_loaded")
        prep, tmin_ready = sem("prep"), sem("tmin_ready")
        held = sem("held")
        prep2, bias_sum = sem("prep2"), sem("bias_sum")
        wa_ready, tmin_mm, part_ready = sem("wa_ready"), sem("tmin_mm"), sem("part_ready")

        with nc.Block() as block:
            @block.sync
            def _(sp):
                for i in range(XL):
                    sp.dma_start(x_all[:, i * XB:(i + 1) * XB, :],
                                 x[i * XB * P:(i + 1) * XB * P, :].rearrange("(b p) d -> p b d", p=P)
                                 ).then_inc(x_loaded[i], 16)
                sp.wait_ge(stT_ready, 1)
                for i, line in enumerate((s_line, t_line)):
                    sp.dma_start(line.rearrange("(b p) -> b p", p=P), st_out[0:L, i, :]).then_inc(line_stored, 16)
                sp.wait_ge(line_stored, 32)
                sp.dma_start(t_row[:, :], t_line.rearrange("(o n) -> o n", o=1).to_broadcast([P, N])).then_inc(line_loaded, 16)
                s_kl = s_line.rearrange("(k l) -> k l", l=L)
                sp.dma_start(s_perm[:, 0:WARM], s_kl[:, OFF:L]).then_inc(line_loaded, 16)
                sp.dma_start(s_perm[:, WARM:L], s_kl[:, 0:OFF]).then_inc(line_loaded, 16)
                sp.wait_ge(line_loaded, 48)

            @block.scalar
            def _(act):
                act.dma_start(w_sb[:, :, 0:D], w_gnn.rearrange("(k p) d -> p k d", p=P)).then_inc(w_loaded, 16)
                act.dma_start(a_row, a_pair.rearrange("(o a d) c -> o a (d c)", o=1, a=2).to_broadcast([P, 2, D])).then_inc(w_loaded, 16)
                act.dma_start(wih[:, :, :], w_ih_t.rearrange("(k p) g -> p k g", p=P)).then_inc(row_loaded, 16)
                act.dma_start(whh[:, :, :], w_hh_t.rearrange("(k p) g -> p k g", p=P)).then_inc(row_loaded, 16)
                act.dma_start(bias[:, :], b_ih.rearrange("(o g) -> o g", o=1).to_broadcast([P, G4])).then_inc(row_loaded, 16)
                act.dma_start(xp[:, :], b_hh.rearrange("(o g) -> o g", o=1).to_broadcast([P, G4])).then_inc(row_loaded, 16)
                act.dma_start(fb[:, 0, :], fw.to_broadcast([P, D])).then_inc(row_loaded, 16)
                act.dma_start(fb[:, 1, :], bw.to_broadcast([P, D])).then_inc(row_loaded, 16)
                act.dma_start(BL, b_lin.rearrange("(o g) -> o g", o=1).to_broadcast([P, 2])).then_inc(row_loaded, 16)
                act.dma_start(wl[:, :, :], w_lin_t.rearrange("(k p) g -> p k g", p=P)).then_inc(row_loaded, 16)
                with act.Fori(0, L // 2) as i:
                    for u in range(2):
                        act.wait_ge(hnT_mm, 2 * i + u + 1)
                        nc.scalar.copy(hnT[:, u, :, :].rearrange("p k q -> p (k q)"), ps_t[u][:, 0:D]).then_inc(hnT_ready, 1)

            @block.gpsimd
            def _(pool):
                nc.gpsimd.memset(ones, 1.0).then_inc(consts, 1)
                nc.gpsimd.memset(ident[:, :], 1.0).then_inc(consts, 1)
                nc.gpsimd.memset(MHALF, -0.5).then_inc(consts, 1)
                nc.gpsimd.memset(half_all, -0.5).then_inc(consts, 1)
                pool.wait_ge(consts, 4)
                nc.gpsimd.affine_select(out=ident[:, :], in_=ident[:, :], compare_op=ALU.is_equal, fill=0.0,
                                        base=0, pattern=[[-1, P]], channel_multiplier=1).then_inc(consts, 1)
                pool.wait_ge(rs_in, 1)
                nc.gpsimd.tensor_tensor(rstd_all, rstd_all, half_all, ALU.pow).then_inc(rs_done, 1)
                nc.gpsimd.memset(part_sum, 0.0).then_inc(part_ready, 1)
                with pool.Fori(0, L) as b:
                    pool.wait_ge(wh_ready, b + 1)
                    hold(pool)
                    pool.wait_ge(part_ready, b + 1)
                    hold(pool)
                    nc.gpsimd.tensor_tensor(part_sum, part_sum, wh[:, bass.ds(b, 1), :].rearrange("p o d -> p (o d)"),
                                            ALU.add).then_inc(part_ready, 1)

            @block.vector
            def _(dve):
                for b in range(L):
                    if b % XB == 0:
                        dve.wait_ge(x_loaded[b // XB], 16)
                    nc.vector.bn_stats(stat_all[:, 6 * b:6 * b + 6], x_all[:, b, :]).then_inc(st_done, 1)
                for b in range(L):
                    dve.wait_ge(st_done, b + 1)
                    nc.vector.bn_aggr(mv_all[:, 2 * b:2 * b + 2], stat_all[:, 6 * b:6 * b + 6]).then_inc(ag_done, 1)
                dve.wait_ge(ag_done, L)
                dve.wait_ge(consts, 5)
                nc.vector.tensor_scalar(rstd_all, mv_all.rearrange("p (b c) -> p b c", c=2)[:, :, 1], EPS, None,
                                        ALU.add).then_inc(rs_in, 1)
                dve.wait_ge(rs_done, 1)
                dve.wait_ge(w_loaded, 32)
                for k in range(KD):
                    for h in range(2):
                        nc.vector.scalar_tensor_tensor(out=dump[:, h, :], in0=w_sb[:, k, 0:D], scalar=1.0, in1=a_row[:, h, :], op0=ALU.mult,
                                                       op1=ALU.mult, accum_out=w_sb[:, k, D + h:D + h + 1]).then_inc(wa_ready, 1)
                        dve.wait_ge(wa_ready, 2 * k + h + 1)

                def norm(b, u):
                    nc.vector.tensor_scalar(hn[:, u, :], x_all[:, bass.ds(b, 1), :].rearrange("p o d -> p (o d)"),
                                            mv_all[:, bass.ds(2 * b, 1)], rstd_all[:, bass.ds(b, 1)],
                                            ALU.subtract, ALU.mult).then_inc(hn_ready, 1)

                def take(b, u):
                    dve.wait_ge(wh_mm, b + 1)
                    hold(dve)
                    nc.vector.tensor_copy(wh[:, bass.ds(b, 1), :].rearrange("p o d -> p (o d)"), ps_o[u][:, 0:D]).then_inc(wh_ready, 1)
                    nc.vector.tensor_copy(st_cols[:, :, bass.ds(b, 1)].rearrange("p a o -> p (a o)"), ps_o[u][:, D:WX]).then_inc(st_ready, 1)

                norm(0, 0)
                norm(1, 1)
                with dve.Fori(0, L // 2 - 1) as i:
                    for u in range(2):
                        take(2 * i + u, u)
                        norm(2 * i + 2 + u, u)
                take(L - 2, 0)
                take(L - 1, 1)
                dve.wait_ge(st_ready, L)
                nc.vector.tensor_reduce(out=Z1, in_=st_cols[:, 1, :], axis=AX.X, op=ALU.min).then_inc(tmin_ready, 1)
                dve.wait_ge(tmin_mm, 1)
                nc.vector.tensor_reduce(out=TMIN[0:1, :], in_=ps_x[0:1, 0:P], axis=AX.X, op=ALU.min).then_inc(tmin_ready, 1)
                dve.wait_ge(tmin_mm, 2)
                nc.vector.tensor_copy(Z2, ps_x[:, P:P + 1]).then_inc(tmin_ready, 1)
                dve.wait_ge(tmin_ready, 3)
                nc.vector.tensor_scalar(st_cols[:, 1, :], st_cols[:, 1, :], Z2, 1.0, ALU.subtract, ALU.add)
                nc.vector.tensor_scalar(st_cols[:, 0, :], st_cols[:, 0, :], Z2, -1.0, ALU.add, ALU.add).then_inc(prep2, 1)
                dve.wait_ge(stT_mm, 1)
                nc.vector.tensor_copy(st_out[0:L, :, :], ps_h[0:L, 0:2 * P].rearrange("p (a b) -> p a b", a=2)).then_inc(stT_ready, 1)
                dve.wait_ge(row_loaded, 8 * 16)
                for t, scale in ((wih, 1.0), (whh, 0.5)):
                    for lo, hi, f in ((0, 2 * D, 0.5), (2 * D, 3 * D, 1.0), (3 * D, G4, 0.5)):
                        if scale * f != 1.0:
                            nc.vector.tensor_scalar(t[:, :, lo:hi], t[:, :, lo:hi], scale * f, None, ALU.mult)
                nc.vector.tensor_scalar(wl[:, :, :], wl[:, :, :], 0.5, None, ALU.mult)
                nc.vector.tensor_scalar(fb[:, :, :], fb[:, :, :], 0.5, None, ALU.mult)
                nc.vector.tensor_tensor(bias[:, :], bias[:, :], xp[:, :], ALU.add).then_inc(bias_sum, 1)
                dve.wait_ge(bias_sum, 1)
                nc.vector.tensor_scalar(bias[:, 0:2 * D], bias[:, 0:2 * D], 0.5, None, ALU.mult)
                nc.vector.tensor_scalar(bias[:, 3 * D:G4], bias[:, 3 * D:G4], 0.5, None, ALU.mult)
                nc.vector.memset(hT[:, :, :], 0.0)
                nc.vector.memset(c2[:, :], 0.0)
                nc.vector.memset(S2[:, :, :], 0.0)
                dve.wait_ge(cs_mm, 1)
                nc.vector.tensor_copy(csum[:, :], ps_g[0][:, 0:D])

            @block.tensor
            def _(pe):
                pe.wait_ge(consts, 5)
                pe.wait_ge(w_loaded, 32)

                def turn(b, u):
                    pe.wait_ge(hn_ready, b + 1)
                    for k in range(KD):
                        last = nc.tensor.transpose(ps_t[u][:, k * P:(k + 1) * P], hn[:, u, k * P:(k + 1) * P], ident[:, :])
                    last.then_inc(hnT_mm, 1)

                def product(b, u):
                    pe.wait_ge(hnT_ready, b + 1)
                    if not isinstance(b, int):
                        pe.wait_ge(st_ready, b - 1)
                    for k in range(KD):
                        last = nc.tensor.matmul(ps_o[u][:, 0:WX], hnT[:, u, k, :], w_sb[:, k, :], start=k == 0, stop=k == KD - 1)
                    last.then_inc(wh_mm, 1)

                pe.wait_ge(wa_ready, 2 * KD)
                turn(0, 0)
                turn(1, 1)
                product(0, 0)
                product(1, 1)
                with pe.Fori(0, L // 2 - 1) as i:
                    turn(2 * i + 2, 0)
                    turn(2 * i + 3, 1)
                    product(2 * i + 2, 0)
                    product(2 * i + 3, 1)
                pe.wait_ge(tmin_ready, 1)
                nc.tensor.matmul(ps_x[0:1, 0:P], Z1, ident[:, :], start=True, stop=True).then_inc(tmin_mm, 1)
                pe.wait_ge(tmin_ready, 2)
                nc.tensor.matmul(ps_x[:, P:P + 1], ones[0:1, :], TMIN[0:1, :], start=True, stop=True).then_inc(tmin_mm, 1)
                pe.wait_ge(prep2, 1)
                for k in range(2):
                    last = nc.tensor.transpose(ps_h[0:L, k * P:(k + 1) * P], st_cols[:, k, :], ident[:, :])
                last.then_inc(stT_mm, 1)
                pe.wait_ge(part_ready, L + 1)
                nc.tensor.matmul(ps_g[0][:, 0:D], ones, part_sum, start=True, stop=True).then_inc(cs_mm, 1)


        adj_loaded = [sem("adj_loaded0"), sem("adj_loaded1")]
        xi_loaded = [sem("xi_loaded0"), sem("xi_loaded1")]
        guard_done, guard_max = sem("guard_done"), sem("guard_max")
        y_ready, y_sum, e_ready, p_ready = sem("y_ready"), sem("y_sum"), sem("e_ready"), sem("p_ready")
        turned, pt_ready, acc_ready = sem("turned"), sem("pt_ready"), sem("acc_ready")
        fin, elu_ready, rstd_ready, x1_stored = sem("fin"), sem("elu_ready"), sem("rstd_ready"), sem("x1_stored")
        xnT_mm, xnT_ready = sem("xnT_mm"), sem("xnT_ready")
        in_mm, in_ready, in_stored = sem("in_mm"), sem("in_ready"), sem("in_stored")
        rec_mm, gate_sum, gate_act = sem("rec_mm"), sem("gate_sum"), sem("gate_act")
        cell, cell_act, h_ready = sem("cell"), sem("cell_act"), sem("h_ready")
        hT_mm, hT_ready = sem("hT_mm"), sem("hT_ready")
        logit_mm, picked = sem("logit_mm"), sem("picked")
        part_a, base_ready, base_stored = sem("part_a"), sem("base_ready"), sem("base_stored")
        shift_mm, shifted, shifted_h = sem("shift_mm"), sem("shifted"), sem("shifted_h")
        again_in = [sem("again_in0"), sem("again_in1")]
        shift_made, end_stored = sem("shift_made"), sem("end_stored")
        x1_free, x1_added = sem("x1_free"), sem("x1_added")
        FIN = 16
        LEAD = 3

        def at(n, per, k):
            return n * per + k

        def tiles(eng, body):
            body(0, 0, True, None, 0)
            with eng.Fori(0, WARM // 2) as i:
                for u in range(2):
                    body(2 * i + 1 + u, (1 + u) % 2, True, "warm", 0)
            yield
            body(WARM + 1, 1, True, "main", 0)
            body(WARM + 2, 0, True, "main", 1)
            with eng.Fori(0, (L - 4 - WARM) // 2) as i:
                for u in range(2):
                    body(2 * i + WARM + 3 + u, (1 + u) % 2, True, "main", 2)
            body(L - 1, 1, False, "main", 2)

        with nc.Block() as block:
            @block.sync
            def _(sp):
                def load(n, position, u, first=False):
                    for c in range(NCH):
                        if not (first and c < 2):
                            sp.wait_ge(guard_done, at(n, NCH, c - 1))
                        sp.dma_start(adj_sb[:, c % 2, :],
                                     adj_kl[:, bass.ds(position, 1), c * CHUNK:(c + 1) * CHUNK].rearrange("k o j -> k (o j)")
                                     ).then_inc(adj_loaded[c % 2], 16)
                    if not first:
                        sp.wait_ge(fin, FIN * n - (2 * FIN - 8))
                    sp.dma_start(x_in[:, u, :], x_kl[:, bass.ds(position, 1), :].rearrange("k o d -> k (o d)")).then_inc(xi_loaded[u], 16)

                load(0, OFF, 0, True)
                for c in range(NCH):
                    sp.wait_ge(guard_done, NCH + c - 1)
                    sp.dma_start(adj_sb[:, c % 2, :], adj_kl[:, OFF + 1, c * CHUNK:(c + 1) * CHUNK]).then_inc(adj_loaded[c % 2], 16)
                sp.dma_start(x_in[:, 1, :], x_kl[:, OFF + 1, :]).then_inc(xi_loaded[1], 16)
                with sp.Fori(0, WARM // 2 - 1) as i:
                    for u in range(2):
                        load(2 * i + 2 + u, 2 * i + (OFF + 2 + u), u)
                with sp.Fori(0, (L - WARM) // 2) as i:
                    for u in range(2):
                        load(2 * i + WARM + u, 2 * i + u, u)
                sp.wait_ge(p_ready, NP * L)
                sp.wait_ge(in_stored, 16 * L)
                sp.wait_ge(x1_stored, 16 * L)
                for r in range(WARM):
                    if r >= 2:
                        sp.wait_ge(h_ready, L + r - 1)
                        sp.wait_ge(base_ready, L + r - WARM)
                    sp.dma_start(xp_again[r % 2], xp_dram[:, OFF + r, :]).then_inc(again_in[r % 2], 16)
                    sp.dma_start(x1_again[r % 2], x1_dram[:, OFF + r, :]).then_inc(again_in[r % 2], 16)

            @block.gpsimd
            def _(pool):
                pool.sem_inc(x1_free, 1)
                pool.sem_inc(x1_added, 1)
                pool.sem_inc(base_ready, 1)
                pool.sem_inc(gate_sum, 2)
                pool.sem_inc(hT_ready, 1)
                pool.sem_inc(picked, 3)
                nc.gpsimd.memset(shift[:, :], 1.0).then_inc(shift_made, 1)
                pool.wait_ge(shift_made, 1)
                nc.gpsimd.affine_select(out=shift[:, :], in_=shift[:, :], compare_op=ALU.is_equal, fill=0.0,
                                        base=1, pattern=[[-1, P]], channel_multiplier=1).then_inc(shift_made, 1)

                def finish_x(m, position):
                    pool.wait_ge(fin, at(m, FIN, 12))
                    hold(pool)
                    pool.dma_start(x1_dram[:, bass.ds(position, 1), :].rearrange("k o d -> k (o d)"), x1[:, :]).then_inc(x1_stored, 16)

                def finish_rstd(m):
                    pool.wait_ge(fin, at(m, FIN, 15))
                    nc.gpsimd.tensor_tensor(RSTD, VE, MHALF, ALU.pow).then_inc(rstd_ready, 1)

                def finish_in(m, position):
                    pool.wait_ge(x1_stored, at(m, 16, 16))
                    pool.sem_inc(x1_free, 1)
                    pool.wait_ge(in_ready, at(m, 2, 2))
                    hold(pool)
                    pool.dma_start(xp_dram[:, bass.ds(position, 1), :].rearrange("k o g -> k (o g)"), xp[:, :]).then_inc(in_stored, 16)

                def forward_part(mm, u, x1=x1[:, :]):
                    if not (isinstance(mm, int) and mm == 0):
                        pool.wait_ge(base_stored, at(mm, 16, 0))
                    pool.wait_ge(picked, at(mm, 3, 6))
                    nc.gpsimd.tensor_tensor(base[:, :], x1, h2[:, :], ALU.add).then_inc(x1_added, 1)
                    nc.gpsimd.tensor_tensor(w3[:, :], S2[:, u, :], fb[:, 0, :], ALU.mult).then_inc(part_a, 1)
                    pool.wait_ge(x1_added, at(mm, 1, 2))
                    hold(pool)
                    pool.wait_ge(part_a, at(mm, 3, 1))
                    nc.gpsimd.tensor_tensor(base[:, :], base[:, :], w3[:, :], ALU.add).then_inc(part_a, 1)

                def backward_part(mm, u):
                    pool.wait_ge(part_a, at(mm, 3, 2))
                    nc.gpsimd.tensor_tensor(w3[:, :], S2[:, 1 - u, :], fb[:, 1, :], ALU.mult).then_inc(part_a, 1)
                    pool.wait_ge(part_a, at(mm, 3, 3))
                    nc.gpsimd.tensor_tensor(base[:, :], base[:, :], w3[:, :], ALU.subtract).then_inc(base_ready, 1)

                def store_base(mm, position):
                    pool.wait_ge(base_ready, at(mm, 1, 2))
                    hold(pool)
                    pool.dma_start(base_dram[:, bass.ds(position, 1), :].rearrange("k o d -> k (o d)"), base[:, :]).then_inc(base_stored, 16)

                def output(mm, u, position, x1=x1[:, :]):
                    forward_part(mm, u, x1)
                    backward_part(mm, u)
                    store_base(mm, position)

                def scores(n, p):
                    pool.wait_ge(y_ready, at(n, NP, p + 1))
                    slot = E[:, p % E_SLOTS, :]
                    nc.gpsimd.tensor_tensor(slot, slot, t_row[:, p * PIECE:(p + 1) * PIECE], ALU.add).then_inc(y_sum, 1)

                when = {0: (3,), 1: (4,), 2: (1,), 3: (0, 5), 5: (2,)}

                def turn(n, u, more, prev, late):
                    for p in range(NP):
                        q = p + LEAD
                        if q < NP:
                            scores(n, q)
                        elif more:
                            scores(n + 1, q - NP)
                        if prev:
                            m, v = n - 1, 1 - u
                            mm = m - WARM if prev == "main" else None
                            position = m - WARM if prev == "main" else m + OFF
                            for k in when.get(p, ()):
                                if k == 0:
                                    finish_x(m, position)
                                elif k == 1:
                                    finish_rstd(m)
                                elif k == 2:
                                    finish_in(m, position)
                                elif late and k == 3:
                                    forward_part(mm - 1, u)
                                elif late and k == 4:
                                    backward_part(mm - 1, u)
                                elif late and k == 5:
                                    store_base(mm - 1, position - 1)

                for p in range(LEAD):
                    scores(0, p)
                for _ in tiles(pool, turn):
                    pass
                output(L - 2 - WARM, 0, OFF - 2)
                finish_x(L - 1, OFF - 1)
                finish_rstd(L - 1)
                finish_in(L - 1, OFF - 1)
                output(L - 1 - WARM, 1, OFF - 1)
                with pool.Fori(0, WARM // 2) as i:
                    for u in range(2):
                        output(2 * i + (L - WARM + u), u, 2 * i + (OFF + u), x1_again[u])
                pool.wait_ge(base_stored, 16 * L)
                pool.wait_ge(x1_stored, 16 * L)
                pool.wait_ge(in_stored, 16 * L)

            @block.scalar
            def _(act):
                def scores(n, u, p):
                    if p == 0:
                        act.wait_ge(guard_max, at(n, 6, 6))
                    if not (isinstance(n, int) and n == 0 and p < E_SLOTS):
                        act.wait_ge(turned, at(n, NG, GPP * (p - E_SLOTS + 1)))
                    nc.scalar.activation(E[:, p % E_SLOTS, :], t_row[:, p * PIECE:(p + 1) * PIECE], ACT.Relu,
                                         bias=BIAS1[u], scale=1.0 / SLOPE - 1.0).then_inc(y_ready, 1)

                def exponentials(n, u, p):
                    act.wait_ge(y_sum, at(n, NP, p + 1))
                    slot = E[:, p % E_SLOTS, :]
                    nc.scalar.activation(slot, slot, ACT.Exp, bias=BIAS2[u], scale=SLOPE).then_inc(e_ready, 1)

                def collect(n, g):
                    act.wait_ge(turned, at(n, NG, g + 1))
                    nc.scalar.copy(PT[:, g % 2, :], ps_t[g % 2][:, :]).then_inc(pt_ready, 1)

                def gates(m, xp=xp[:, :]):
                    act.wait_ge(gate_sum, at(m, 2, 4))
                    nc.scalar.activation(xp, xp, ACT.Tanh).then_inc(gate_act, 1)

                def cell_out(m):
                    act.wait_ge(cell, at(m, 3, 3))
                    nc.scalar.activation(w1[:, :], c2[:, :], ACT.Tanh, scale=0.5).then_inc(cell_act, 1)

                def state_turned(m):
                    act.wait_ge(hT_mm, at(m, 1, 1))
                    nc.scalar.copy(hT[:, :, :].rearrange("p k q -> p (k q)"), ps_h[:, 0:D]).then_inc(hT_ready, 1)

                when = {2: 0, 6: 1, 12: 2, 13: 3, 14: 4}

                def turn(n, u, more, prev, late):
                    for g in range(NG):
                        part, p = (scores, exponentials)[g % GPP], g // GPP + LEAD
                        if g % GPP == 1:
                            collect(n, g)
                        if p < NP:
                            part(n, u, p)
                        elif more:
                            part(n + 1, 1 - u, p - NP)
                        if g % GPP == 0:
                            collect(n, g)
                        if prev:
                            for h, k in when.items():
                                if h == g:
                                    m, v = n - 1, 1 - u
                                    if k == 0:
                                        act.wait_ge(fin, at(m, FIN, 7))
                                        nc.scalar.activation(w2[:, :], w2[:, :], ACT.Tanh, scale=0.5).then_inc(elu_ready, 1)
                                    elif k == 1:
                                        act.wait_ge(xnT_mm, at(m, 1, 1))
                                        nc.scalar.copy(xnT[:, :, :].rearrange("p k q -> p (k q)"), ps_x[:, 0:D]).then_inc(xnT_ready, 1)
                                    elif k == 2:
                                        gates(m)
                                    elif k == 3:
                                        cell_out(m)
                                    else:
                                        state_turned(m)

                for p in range(LEAD):
                    scores(0, 0, p)
                for p in range(LEAD):
                    exponentials(0, 0, p)
                for _ in tiles(act, turn):
                    act.wait_ge(h_ready, WARM)
                    act.dma_start(end_dram[0], h2[:, :]).then_inc(end_stored, 16)
                    act.dma_start(end_dram[1], c2[:, :]).then_inc(end_stored, 16)
                    act.wait_ge(shift_mm, 1)
                    nc.scalar.copy(hT[:, :, :].rearrange("p k q -> p (k q)"), ps_h[:, 0:D]).then_inc(shifted_h, 1)
                m = L - 1
                act.wait_ge(fin, at(m, FIN, 7))
                nc.scalar.activation(w2[:, :], w2[:, :], ACT.Tanh, scale=0.5).then_inc(elu_ready, 1)
                act.wait_ge(xnT_mm, m + 1)
                nc.scalar.copy(xnT[:, :, :].rearrange("p k q -> p (k q)"), ps_x[:, 0:D]).then_inc(xnT_ready, 1)

                def step(m, xp=xp[:, :]):
                    gates(m, xp)
                    cell_out(m)
                    state_turned(m)
                step(L - 1)
                with act.Fori(0, WARM // 2) as i:
                    for u in range(2):
                        step(2 * i + (L + u), xp_again[u])

            @block.vector
            def _(dve):
                def guard(n, u, c):
                    dve.wait_ge(adj_loaded[c % 2], at(n, 16 * NCH // 2, 16 * (c // 2) + 16))
                    hold(dve)
                    nc.vector.tensor_tensor_reduce(out=nb[:, u, c * CHUNK:(c + 1) * CHUNK], in0=adj_sb[:, c % 2, :],
                                                   in1=t_row[:, c * CHUNK:(c + 1) * CHUNK], scale=1.0, scalar=0.0,
                                                   op0=ALU.mult, op1=ALU.max, accum_out=gmx[:, u, c:c + 1]).then_inc(guard_done, 1)

                def row_max(n, u):
                    dve.wait_ge(guard_done, at(n, NCH, NCH))
                    nc.vector.tensor_reduce(out=GM[u], in_=gmx[:, u, :], axis=AX.X, op=ALU.max).then_inc(guard_max, 1)
                    nc.vector.tensor_copy(SC, s_perm[:, bass.ds(n, 1)]).then_inc(guard_max, 1)
                    dve.wait_ge(guard_max, at(n, 6, 2))
                    nc.vector.tensor_tensor(Z1, GM[u], SC, ALU.add).then_inc(guard_max, 1)
                    dve.wait_ge(guard_max, at(n, 6, 3))
                    nc.vector.tensor_scalar(Z2, Z1, -SLOPE, -1.0, ALU.mult, ALU.add)
                    nc.vector.tensor_scalar(Z3, Z1, -1.0, -1.0, ALU.mult, ALU.add).then_inc(guard_max, 1)
                    dve.wait_ge(guard_max, at(n, 6, 4))
                    nc.vector.tensor_tensor(NEGM, Z2, Z3, ALU.min).then_inc(guard_max, 1)
                    dve.wait_ge(guard_max, at(n, 6, 5))
                    nc.vector.tensor_scalar(BIAS1[u], SC, 1.0 / SLOPE - 1.0, None, ALU.mult)
                    nc.vector.scalar_tensor_tensor(out=BIAS2[u], in0=SC, scalar=SLOPE, in1=NEGM, op0=ALU.mult,
                                                   op1=ALU.add).then_inc(guard_max, 1)

                def weights(n, u, p):
                    e = E[:, p % E_SLOTS, :]
                    dve.wait_ge(e_ready, at(n, NP, p + 1))
                    nc.vector.scalar_tensor_tensor(out=e, in0=nb[:, u, p * PIECE:(p + 1) * PIECE], scalar=0.0, in1=e,
                                                   op0=ALU.is_gt, op1=ALU.min, accum_out=rs[:, u, p:p + 1]).then_inc(p_ready, 1)

                def counted(m, first):
                    k = [first]

                    def step(ins, wait=True):
                        k[0] += 1
                        ins.then_inc(fin, 1)
                        if wait:
                            dve.wait_ge(fin, at(m, FIN, k[0]))
                    return step

                def divide(m, u):
                    step, v = counted(m, 0), nc.vector
                    dve.wait_ge(p_ready, at(m, NP, NP))
                    step(v.tensor_reduce(out=RSUM, in_=rs[:, u, :], axis=AX.X, op=ALU.add), False)
                    step(v.tensor_scalar(NONE, GM[u], 0.0, None, ALU.is_le))
                    step(v.scalar_tensor_tensor(out=DEN, in0=NONE, scalar=float(N), in1=RSUM, op0=ALU.mult, op1=ALU.add))
                    step(v.reciprocal(RINV, DEN), False)
                    dve.wait_ge(acc_ready, at(m, 1, 1))
                    step(v.scalar_tensor_tensor(out=w1b[:, :], in0=csum[:, :], scalar=NONE, in1=ps_o[u][:, 0:D], op0=ALU.mult, op1=ALU.add))
                    step(v.tensor_scalar(w1b[:, :], w1b[:, :], RINV, None, ALU.mult))
                    step(v.tensor_scalar(w2[:, :], w1b[:, :], 0.0, None, ALU.min), False)
                    dve.wait_ge(xi_loaded[u], at(m, 8, 16 - 8 * u))
                    step(v.scalar_tensor_tensor(out=w1b[:, :], in0=w1b[:, :], scalar=0.0, in1=x_in[:, u, :], op0=ALU.max, op1=ALU.add), False)

                def normalise(m, mm):
                    step, v = counted(m, 8), nc.vector
                    dve.wait_ge(elu_ready, at(m, 1, 1))
                    step(v.tensor_scalar(xn[:, :], w2[:, :], -1.0, 1.0, ALU.mult, ALU.add))
                    step(v.reciprocal(xn[:, :], xn[:, :]))
                    step(v.scalar_tensor_tensor(out=w2[:, :], in0=w2[:, :], scalar=2.0, in1=xn[:, :], op0=ALU.mult, op1=ALU.mult))
                    dve.wait_ge(x1_free, at(m, 1, 1))
                    if mm is not None:
                        dve.wait_ge(x1_added, at(mm, 1, 1))
                    step(v.tensor_tensor(x1[:, :], w1b[:, :], w2[:, :], ALU.add))
                    step(v.bn_stats(STATS, x1[:, :]))
                    hold(dve)
                    step(v.bn_aggr(MV, STATS))
                    step(v.tensor_scalar(VE, MV[:, 1:2], EPS, None, ALU.add), False)

                def normalised(m):
                    step, v = counted(m, 15), nc.vector
                    dve.wait_ge(rstd_ready, at(m, 1, 1))
                    step(v.tensor_scalar(xn[:, :], x1[:, :], MV[:, 0:1], RSTD, ALU.subtract, ALU.mult), False)

                def inputs(m):
                    for h in range(2):
                        dve.wait_ge(in_mm, at(m, 2, h + 1))
                        nc.vector.tensor_tensor(xp[:, h * HALF:(h + 1) * HALF], ps_g[h][:, :], bias[:, h * HALF:(h + 1) * HALF],
                                                ALU.add).then_inc(in_ready, 1)

                def gates(m, xp=xp, stored=True):
                    if stored:
                        dve.wait_ge(in_stored, at(m, 16, 16))
                    for h in range(2):
                        dve.wait_ge(rec_mm, at(m, 2, h + 1))
                        half = xp[:, h * HALF:(h + 1) * HALF]
                        nc.vector.tensor_tensor(half, half, ps_g[h][:, :], ALU.add).then_inc(gate_sum, 1)

                def new_cell(m, xp=xp):
                    dve.wait_ge(gate_act, at(m, 1, 1))
                    nc.vector.scalar_tensor_tensor(out=w1b[:, :], in0=xp[:, D:2 * D], scalar=1.0, in1=c2[:, :],
                                                   op0=ALU.add, op1=ALU.mult).then_inc(cell, 1)
                    nc.vector.scalar_tensor_tensor(out=xn[:, :], in0=xp[:, 0:D], scalar=1.0, in1=xp[:, 2 * D:3 * D],
                                                   op0=ALU.add, op1=ALU.mult).then_inc(cell, 1)
                    dve.wait_ge(cell, at(m, 3, 2))
                    nc.vector.scalar_tensor_tensor(out=c2[:, :], in0=w1b[:, :], scalar=0.5, in1=xn[:, :],
                                                   op0=ALU.mult, op1=ALU.add).then_inc(cell, 1)

                def new_state(m, mm, xp=xp):
                    if mm is not None:
                        dve.wait_ge(base_ready, at(mm, 1, 1))
                    dve.wait_ge(cell_act, at(m, 1, 1))
                    nc.vector.scalar_tensor_tensor(out=h2[:, :], in0=xp[:, 3 * D:G4], scalar=1.0, in1=w1[:, :],
                                                   op0=ALU.add, op1=ALU.mult).then_inc(h_ready, 1)

                def pick(mm, u):
                    dve.wait_ge(logit_mm, at(mm, 1, 1))
                    nc.vector.tensor_scalar(LD, ps_h[:, 0:1], BL[:, 0:1], None, ALU.add).then_inc(picked, 1)
                    dve.wait_ge(picked, at(mm, 3, 4))
                    nc.vector.tensor_scalar(LG, ps_h[:, 1:2], BL[:, 1:2], LD, ALU.add, ALU.is_gt).then_inc(picked, 1)
                    dve.wait_ge(picked, at(mm, 3, 5))
                    nc.vector.scalar_tensor_tensor(out=S2[:, 1 - u, :], in0=h2[:, :], scalar=LG, in1=S2[:, u, :],
                                                   op0=ALU.mult, op1=ALU.add).then_inc(picked, 1)

                guard_at = (0, 1, 3, 4)
                when = {0: (5,), 1: (0,), 2: (1,), 3: (6,), 5: (2,), 7: (3, 4)}

                def turn(n, u, more, prev, late):
                    for p in range(NP):
                        weights(n, u, p)
                        if prev:
                            m, v = n - 1, 1 - u
                            mm = m - WARM if prev == "main" else None
                            for k in when.get(p, ()):
                                if k == 0:
                                    divide(m, v)
                                elif k == 1:
                                    normalise(m, mm)
                                elif k == 6:
                                    normalised(m)
                                elif k == 2:
                                    inputs(m)
                                elif k == 3:
                                    gates(m)
                                elif k == 4:
                                    new_cell(m)
                                    new_state(m, mm)
                                elif late:
                                    pick(mm - 1, u)
                        if more and p in guard_at:
                            guard(n + 1, 1 - u, guard_at.index(p))
                        if more and p == 5:
                            row_max(n + 1, 1 - u)

                for c in range(NCH):
                    guard(0, 0, c)
                row_max(0, 0)
                for _ in tiles(dve, turn):
                    dve.wait_ge(end_stored, 32)
                    dve.wait_ge(shift_mm, 1)
                    nc.vector.tensor_copy(c2[:, :], ps_x[:, D:2 * D]).then_inc(shifted, 1)
                pick(L - 2 - WARM, 0)
                divide(L - 1, 1)
                normalise(L - 1, L - 1 - WARM)
                normalised(L - 1)
                inputs(L - 1)
                gates(L - 1)
                new_cell(L - 1)
                new_state(L - 1, L - 1 - WARM)
                pick(L - 1 - WARM, 1)
                with dve.Fori(0, WARM // 2) as i:
                    for u in range(2):
                        m, mm = 2 * i + (L + u), 2 * i + (L - WARM + u)
                        dve.wait_ge(again_in[u], 32 * i + 32)
                        gates(m, xp_again[u], False)
                        new_cell(m, xp_again[u])
                        new_state(m, mm, xp_again[u])
                        pick(mm, u)

            @block.tensor
            def _(pe):
                def turned_group(n, g):
                    if g % GPP == 0:
                        pe.wait_ge(p_ready, at(n, NP, g // GPP + 1))
                    p, first = g // GPP, g % GPP * GROUP
                    for b in range(BPG):
                        last = nc.tensor.transpose(ps_t[g % 2][:, b * P:(b + 1) * P],
                                                   E[:, p % E_SLOTS, first + b * P:first + (b + 1) * P], ident[:, :])
                    last.then_inc(turned, 1)

                def summed_group(n, u, g):
                    pe.wait_ge(pt_ready, at(n, NG, g + 1))
                    for b in range(BPG):
                        last = nc.tensor.matmul(ps_o[u][:, 0:D], PT[:, g % 2, b * P:(b + 1) * P], wh[:, g * BPG + b, :],
                                                start=g == 0 and b == 0, stop=g == NG - 1 and b == BPG - 1)
                    if g == NG - 1:
                        last.then_inc(acc_ready, 1)

                def x_turned(m):
                    pe.wait_ge(fin, at(m, FIN, 16))
                    for k in range(KD):
                        last = nc.tensor.transpose(ps_x[:, k * P:(k + 1) * P], xn[:, k * P:(k + 1) * P], ident[:, :])
                    last.then_inc(xnT_mm, 1)

                def x_product(m):
                    pe.wait_ge(xnT_ready, at(m, 1, 1))
                    pe.wait_ge(gate_sum, at(m, 2, 2))
                    for h in range(2):
                        for k in range(KD):
                            last = nc.tensor.matmul(ps_g[h][:, :], xnT[:, k, :], wih[:, k, h * HALF:(h + 1) * HALF], start=k == 0, stop=k == KD - 1)
                        last.then_inc(in_mm, 1)

                def h_product(m, fresh=True):
                    if fresh:
                        pe.wait_ge(in_ready, at(m, 2, 2))
                    else:
                        pe.wait_ge(gate_sum, at(m, 2, 2))
                    pe.wait_ge(hT_ready, at(m, 1, 1))
                    for h in range(2):
                        for k in range(KD):
                            last = nc.tensor.matmul(ps_g[h][:, :], hT[:, k, :], whh[:, k, h * HALF:(h + 1) * HALF], start=k == 0, stop=k == KD - 1)
                        last.then_inc(rec_mm, 1)

                def h_turned(m, mm):
                    pe.wait_ge(h_ready, at(m, 1, 1))
                    if mm is not None:
                        pe.wait_ge(picked, at(mm, 3, 3))
                    for k in range(KD):
                        last = nc.tensor.transpose(ps_h[:, k * P:(k + 1) * P], h2[:, k * P:(k + 1) * P], ident[:, :])
                    last.then_inc(hT_mm, 1)

                def logits(m, mm):
                    pe.wait_ge(hT_ready, at(m, 1, 2))
                    for k in range(KD):
                        last = nc.tensor.matmul(ps_h[:, 0:2], hT[:, k, :], wl[:, k, :], start=k == 0, stop=k == KD - 1)
                    last.then_inc(logit_mm, 1)

                when = {6: (0,), 7: (1,), 10: (2,), 14: (3,), 15: (4,)}

                def turn(n, u, more, prev, late):
                    for g in range(NG):
                        turned_group(n, g)
                        if g > 0:
                            summed_group(n, u, g - 1)
                        elif prev:
                            summed_group(n - 1, 1 - u, NG - 1)
                        if prev:
                            m, v = n - 1, 1 - u
                            mm = m - WARM if prev == "main" else None
                            for k in when.get(g, ()):
                                if k == 0:
                                    x_turned(m)
                                elif k == 1:
                                    x_product(m)
                                elif k == 2:
                                    h_product(m)
                                elif k == 3:
                                    h_turned(m, mm)
                                elif mm is not None:
                                    logits(m, mm)

                for _ in tiles(pe, turn):
                    pe.wait_ge(shift_made, 2)
                    pe.wait_ge(h_ready, WARM)
                    pe.wait_ge(hT_ready, WARM + 1)
                    for k in range(KD):
                        nc.tensor.matmul(ps_h[:, k * P:(k + 1) * P], h2[:, k * P:(k + 1) * P], shift[:, :], start=True, stop=True)
                    nc.tensor.matmul(ps_x[:, D:2 * D], shift[:, :], c2[:, :], start=True, stop=True).then_inc(shift_mm, 1)
                    pe.wait_ge(shifted, 1)
                    pe.wait_ge(shifted_h, 1)
                summed_group(L - 1, 1, NG - 1)
                x_turned(L - 1)
                x_product(L - 1)
                h_product(L - 1)
                h_turned(L - 1, L - 1 - WARM)
                logits(L - 1, L - 1 - WARM)
                with pe.Fori(0, WARM // 2) as i:
                    for u in range(2):
                        m, mm = 2 * i + (L + u), 2 * i + (L - WARM + u)
                        h_product(m, False)
                        h_turned(m, mm)
                        logits(m, mm)

        end_in, differ, differ_max, decided = sem("end_in"), sem("differ"), sem("differ_max"), sem("decided")
        with nc.Block() as block:
            @block.sync
            def _(sp):
                sp.dma_start(x_in[:, 0, :], end_dram[0]).then_inc(end_in, 16)
                sp.dma_start(x_in[:, 1, :], end_dram[1]).then_inc(end_in, 16)

            @block.vector
            def _(dve):
                v = nc.vector
                dve.wait_ge(end_in, 32)
                v.tensor_tensor(x_in[:, 0, :], x_in[:, 0, :], h2[:, :], ALU.subtract)
                v.tensor_tensor(x_in[:, 1, :], x_in[:, 1, :], c2[:, :], ALU.subtract).then_inc(differ, 1)
                dve.wait_ge(differ, 1)
                v.tensor_reduce(out=DMX[:, 0:1], in_=x_in[:, :, :], axis=AX.XY, op=ALU.max,
                                apply_absolute_value=True).then_inc(differ, 1)
                dve.wait_ge(differ_max, 1)
                v.tensor_reduce(out=DMX[0:1, 1:2], in_=ps_x[0:1, 0:P], axis=AX.X, op=ALU.max).then_inc(differ, 1)
                dve.wait_ge(differ, 3)
                v.tensor_scalar(DMX[0:1, 2:3], DMX[0:1, 1:2], TOL, None, ALU.is_le).then_inc(differ, 1)
                dve.wait_ge(differ, 4)
                v.tensor_scalar(flag[0:1, 0:1], DMX[0:1, 2:3], -1.0, 1.0, ALU.mult, ALU.add).then_inc(decided, 1)

            @block.tensor
            def _(pe):
                pe.wait_ge(differ, 2)
                nc.tensor.matmul(ps_x[0:1, 0:P], DMX[:, 0:1], ident[:, :], start=True, stop=True).then_inc(differ_max, 1)

        g_load, g_store = sem("g_load"), sem("g_store")
        g_in, g_step, g_shift = sem("g_in"), sem("g_step"), sem("g_shift")
        g_start_h, g_start_c = sem("g_start_h"), sem("g_start_c")
        g_rec, g_sum, g_act, g_cell, g_cell_act = sem("g_rec"), sem("g_sum"), sem("g_act"), sem("g_cell"), sem("g_cell_act")
        g_h, g_hT_mm, g_hT, g_logit, g_base = sem("g_h"), sem("g_hT_mm"), sem("g_hT"), sem("g_logit"), sem("g_base")

        def sweeps(eng, start, step):
            needed = eng.value_load(flag[0:1, 0:1], min_val=0, max_val=1)
            with eng.If(needed):
                with eng.Fori(0, SWEEPS) as q:
                    start(q)
                    with eng.Fori(0, L) as l:
                        step(q * L + l, l)

        with nc.Block() as block:
            @block.sync
            def _(sp):
                def step(r, l):
                    sp.wait_ge(g_step, r + 1)
                    hold(sp)
                    sp.dma_start(xp_again[0], xp_dram[:, bass.ds(l, 1), :].rearrange("k o g -> k (o g)")).then_inc(g_load, 16)
                    sp.dma_start(x1_again[0], x1_dram[:, bass.ds(l, 1), :].rearrange("k o d -> k (o d)")).then_inc(g_load, 16)
                    sp.wait_ge(g_load, 32)
                    sp.sem_clear(g_load)
                    sp.sem_inc(g_in, 1)
                    sp.wait_ge(g_base, r + 1)
                    hold(sp)
                    sp.dma_start(base_dram[:, bass.ds(l, 1), :].rearrange("k o d -> k (o d)"), base[:, :]).then_inc(g_store, 16)
                    sp.wait_ge(g_store, 16)
                    sp.sem_clear(g_store)
                    sp.sem_inc(g_step, 1)
                sp.sem_inc(g_step, 1)
                sweeps(sp, lambda q: None, step)

            @block.tensor
            def _(pe):
                def start(q):
                    pe.wait_ge(g_step, q * L + 1)
                    for k in range(KD):
                        nc.tensor.matmul(ps_h[:, k * P:(k + 1) * P], h2[:, k * P:(k + 1) * P], shift[:, :], start=True, stop=True)
                    nc.tensor.matmul(ps_x[:, D:2 * D], shift[:, :], c2[:, :], start=True, stop=True).then_inc(g_shift, 1)
                    pe.wait_ge(g_start_h, q + 1)
                    hold(pe)

                def step(r, l):
                    pe.wait_ge(g_step, r + 1)
                    for h in range(2):
                        for k in range(KD):
                            last = nc.tensor.matmul(ps_g[h][:, :], hT[:, k, :], whh[:, k, h * HALF:(h + 1) * HALF], start=k == 0, stop=k == KD - 1)
                    last.then_inc(g_rec, 1)
                    pe.wait_ge(g_h, r + 1)
                    for k in range(KD):
                        last = nc.tensor.transpose(ps_h[:, k * P:(k + 1) * P], h2[:, k * P:(k + 1) * P], ident[:, :])
                    last.then_inc(g_hT_mm, 1)
                    pe.wait_ge(g_hT, r + 1)
                    for k in range(KD):
                        last = nc.tensor.matmul(ps_h[:, 0:2], hT[:, k, :], wl[:, k, :], start=k == 0, stop=k == KD - 1)
                    last.then_inc(g_logit, 1)
                sweeps(pe, start, step)

            @block.scalar
            def _(act):
                def start(q):
                    act.wait_ge(g_shift, q + 1)
                    nc.scalar.copy(hT[:, :, :].rearrange("p k q -> p (k q)"), ps_h[:, 0:D]).then_inc(g_start_h, 1)

                def step(r, l):
                    act.wait_ge(g_sum, r + 1)
                    nc.scalar.activation(xp_again[0], xp_again[0], ACT.Tanh).then_inc(g_act, 1)
                    act.wait_ge(g_cell, r + 1)
                    nc.scalar.activation(w1[:, :], c2[:, :], ACT.Tanh, scale=0.5).then_inc(g_cell_act, 1)
                    act.wait_ge(g_hT_mm, r + 1)
                    nc.scalar.copy(hT[:, :, :].rearrange("p k q -> p (k q)"), ps_h[:, 0:D]).then_inc(g_hT, 1)
                sweeps(act, start, step)

            @block.vector
            def _(dve):
                v = nc.vector
                g = xp_again[0]
                S = S2[:, 0, :]

                def start(q):
                    dve.wait_ge(g_shift, q + 1)
                    v.tensor_copy(c2[:, :], ps_x[:, D:2 * D])
                    v.memset(S, 0.0)
                    dve.drain()

                def step(r, l):
                    dve.wait_ge(g_in, r + 1)
                    hold(dve)
                    dve.wait_ge(g_rec, r + 1)
                    for h in range(2):
                        half = g[:, h * HALF:(h + 1) * HALF]
                        last = v.tensor_tensor(half, half, ps_g[h][:, :], ALU.add)
                    last.then_inc(g_sum, 1)
                    dve.wait_ge(g_act, r + 1)
                    v.scalar_tensor_tensor(out=w1b[:, :], in0=g[:, D:2 * D], scalar=1.0, in1=c2[:, :], op0=ALU.add, op1=ALU.mult)
                    v.scalar_tensor_tensor(out=xn[:, :], in0=g[:, 0:D], scalar=1.0, in1=g[:, 2 * D:3 * D], op0=ALU.add, op1=ALU.mult)
                    dve.drain()
                    v.scalar_tensor_tensor(out=c2[:, :], in0=w1b[:, :], scalar=0.5, in1=xn[:, :], op0=ALU.mult, op1=ALU.add).then_inc(g_cell, 1)
                    dve.wait_ge(g_cell_act, r + 1)
                    v.scalar_tensor_tensor(out=h2[:, :], in0=g[:, 3 * D:G4], scalar=1.0, in1=w1[:, :], op0=ALU.add, op1=ALU.mult).then_inc(g_h, 1)
                    dve.wait_ge(g_logit, r + 1)
                    v.tensor_scalar(LD, ps_h[:, 0:1], BL[:, 0:1], None, ALU.add)
                    v.tensor_tensor(base[:, :], x1_again[0], h2[:, :], ALU.add)
                    v.tensor_tensor(w2[:, :], S, fb[:, 0, :], ALU.mult)
                    dve.drain()
                    v.tensor_scalar(LG, ps_h[:, 1:2], BL[:, 1:2], LD, ALU.add, ALU.is_gt)
                    v.tensor_tensor(base[:, :], base[:, :], w2[:, :], ALU.add)
                    dve.drain()
                    v.scalar_tensor_tensor(out=S, in0=h2[:, :], scalar=LG, in1=S, op0=ALU.mult, op1=ALU.add)
                    dve.drain()
                    v.tensor_tensor(w2[:, :], S, fb[:, 1, :], ALU.mult)
                    dve.drain()
                    v.tensor_tensor(base[:, :], base[:, :], w2[:, :], ALU.subtract).then_inc(g_base, 1)
                sweeps(dve, start, step)

        tot_mm, off_ready, add_ready, base_in = sem("tot_mm"), sem("off_ready"), sem("add_ready"), sem("base_in")
        out_ready, out_stored, tables = sem("out_ready"), sem("out_stored"), sem("tables")
        OB = 8
        OW = L // OB
        with nc.Block() as block:
            @block.gpsimd
            def _(pool):
                nc.gpsimd.memset(strict, 1.0).then_inc(tables, 1)
                nc.gpsimd.memset(ones, 1.0).then_inc(tables, 1)
                pool.wait_ge(tables, 2)
                nc.gpsimd.affine_select(out=strict, in_=strict, compare_op=ALU.is_gt, fill=0.0,
                                        base=0, pattern=[[1, P]], channel_multiplier=-1).then_inc(tables, 1)

            @block.tensor
            def _(pe):
                pe.wait_ge(tables, 3)
                nc.tensor.matmul(ps_x[:, 0:D], strict, S2[:, 0, :], start=True, stop=True)
                nc.tensor.matmul(ps_h[:, 0:D], ones, S2[:, 0, :], start=True, stop=True).then_inc(tot_mm, 1)

            @block.sync
            def _(sp):
                for i in range(OB):
                    sp.dma_start(wh[:, i * OW:(i + 1) * OW, :], base_dram[:, i * OW:(i + 1) * OW, :]).then_inc(base_in, 16)
                for i in range(OB):
                    sp.wait_ge(out_ready, i + 1)
                    sp.dma_start(out_kl[:, i * OW:(i + 1) * OW, :], wh[:, i * OW:(i + 1) * OW, :]).then_inc(out_stored, 16)
                sp.wait_ge(out_stored, 16 * OB)

            @block.vector
            def _(dve):
                v = nc.vector
                dve.wait_ge(tot_mm, 1)
                v.tensor_copy(w1[:, :], ps_x[:, 0:D]).then_inc(off_ready, 1)
                dve.wait_ge(off_ready, 1)
                v.tensor_tensor(w2[:, :], ps_h[:, 0:D], w1[:, :], ALU.subtract).then_inc(off_ready, 1)
                v.tensor_tensor(w1[:, :], w1[:, :], fb[:, 0, :], ALU.mult).then_inc(off_ready, 1)
                dve.wait_ge(off_ready, 2)
                v.tensor_tensor(w2[:, :], w2[:, :], fb[:, 1, :], ALU.mult).then_inc(off_ready, 1)
                dve.wait_ge(off_ready, 4)
                v.tensor_tensor(w1[:, :], w1[:, :], w2[:, :], ALU.add).then_inc(off_ready, 1)
                dve.wait_ge(off_ready, 5)
                for i in range(OB):
                    dve.wait_ge(base_in, 16 * OB)
                    part = wh[:, i * OW:(i + 1) * OW, :]
                    v.tensor_tensor(part, part, w1[:, :].rearrange("p (o d) -> p o d", o=1).to_broadcast([P, OW, D]),
                                    ALU.add).then_inc(out_ready, 1)


def kernel(x, adj, L0_gnn_W, L0_gnn_a, L0_ffn_W_ih, L0_ffn_W_hh, L0_ffn_b_ih, L0_ffn_b_hh, L0_ffn_W_lin,
           L0_ffn_b_lin, L0_ffn_fw_att, L0_ffn_bw_att):
    import numpy as np
    import concourse.bacc as bacc
    from concourse import mybir as mb
    from concourse.bass_utils import run_bass_kernel_spmd as run

    nc = bacc.Bacc("TRN2", target_bir_lowering=False, num_devices=1)
    laid = [("x", x), ("adj", adj), ("w_gnn", L0_gnn_W), ("a_pair", L0_gnn_a), ("w_ih_t", np.asarray(L0_ffn_W_ih).T),
            ("w_hh_t", np.asarray(L0_ffn_W_hh).T), ("b_ih", L0_ffn_b_ih), ("b_hh", L0_ffn_b_hh),
            ("w_lin_t", np.asarray(L0_ffn_W_lin).T), ("b_lin", L0_ffn_b_lin), ("fw", L0_ffn_fw_att), ("bw", L0_ffn_bw_att)]
    arrays, args = {}, []
    for name, a in laid:
        a = np.ascontiguousarray(a)
        arrays[name] = a
        args.append(nc.dram_tensor(name, a.shape, mb.dt.from_np(a.dtype), kind="ExternalInput").ap())
    args.append(nc.dram_tensor("out", x.shape, mb.dt.float32, kind="ExternalOutput").ap())
    adj_ffn_kernel(nc, *args)
    return run(nc, [arrays], core_ids=[0]).results[0]["out"]
```

```python
from contextlib import ExitStack

import concourse.bass as bass
from concourse import mybir

F32 = mybir.dt.float32
BF16 = mybir.dt.bfloat16
I32 = mybir.dt.int32
ALU = mybir.AluOpType
ACT = mybir.ActivationFunctionType
AX = mybir.AxisListType

P = 128
D = 256
KD = D // P
G4 = 4 * D
HALF = G4 // 2
EPS = 1e-5
SLOPE = 0.2
TOL = 2.0 ** -19
CHUNK = 2048
PIECE = 1024
GROUP = 512
E_SLOTS = 4


def adj_ffn_kernel(nc, x, adj, w_gnn, a_pair, w_ih_t, w_hh_t, b_ih, b_hh, w_lin_t, b_lin, fw, bw, out, warm=32, SWEEPS=P - 1):
    N = x.shape[0]
    L = N // P
    NCH, NP, NG = N // CHUNK, N // PIECE, N // GROUP
    BPG = GROUP // P
    GPP = PIECE // GROUP
    WARM = warm
    OFF = L - WARM

    x_kl = x.rearrange("(k l) d -> k l d", l=L)
    adj_kl = adj.rearrange("(k l) j -> k l j", l=L)
    out_kl = out.rearrange("(k l) d -> k l d", l=L)
    t_line = nc.dram_tensor("t_line", [N], F32, kind="Internal").ap()
    s_line = nc.dram_tensor("s_line", [N], F32, kind="Internal").ap()
    xp_dram = nc.dram_tensor("xp_dram", [P, L, G4], F32, kind="Internal").ap()
    x1_dram = nc.dram_tensor("x1_dram", [P, L, D], F32, kind="Internal").ap()
    end_dram = nc.dram_tensor("end_dram", [2, P, D], F32, kind="Internal").ap()
    base_dram = nc.dram_tensor("base_dram", [P, L, D], F32, kind="Internal").ap()

    with ExitStack() as ctx:
        def sb(name, shape, dt=F32):
            return ctx.enter_context(nc.sbuf_tensor(name, shape, dt))

        def pb(name):
            return ctx.enter_context(nc.psum_tensor(name, [P, 512], F32))

        def sem(name):
            return ctx.enter_context(nc.semaphore(name))

        def hold(eng):
            eng.sem_inc(held, 1)

        wh = sb("wh", [P, L, D])
        t_row = sb("t_row", [P, N])
        adj_sb = sb("adj_sb", [P, 2, CHUNK])
        nb = sb("nb", [P, 2, N], BF16)
        E = sb("E", [P, E_SLOTS, PIECE])
        PT = sb("PT", [P, 2, GROUP])
        wih = sb("wih", [P, KD, G4])
        whh = sb("whh", [P, KD, G4])
        bias = sb("bias", [P, G4])
        xp = sb("xp", [P, G4])
        ident = sb("ident", [P, P])
        shift = sb("shift", [P, P])
        w1b = sb("w1b", [P, D])
        w3 = sb("w3", [P, D])
        small = sb("small", [P, 64])
        x_in = sb("x_in", [P, 2, D])
        x1 = sb("x1", [P, D])
        w1 = sb("w1", [P, D])
        w2 = sb("w2", [P, D])
        xn = sb("xn", [P, D])
        xnT = sb("xnT", [P, KD, P])
        hT = sb("hT", [P, KD, P])
        c2 = sb("c2", [P, D])
        h2 = sb("h2", [P, D])
        csum = sb("csum", [P, D])
        S2 = sb("S2", [P, 2, D])
        fb = sb("fb", [P, 2, D])
        base = sb("base", [P, D])
        s_perm = sb("s_perm", [P, L])
        wl = sb("wl", [P, KD, 2])
        rs = sb("rs", [P, 2, NP])
        gmx = sb("gmx", [P, 2, NCH])
        flag = sb("flag", [P, 2], I32)

        ps_t = [pb("ps_t0"), pb("ps_t1")]
        ps_o = [pb("ps_o0"), pb("ps_o1")]
        ps_x, ps_h = pb("ps_x"), pb("ps_h")
        ps_g = [pb("ps_g0"), pb("ps_g1")]

        def col(k, n=1):
            return small[:, k:k + n]
        BL, TMIN, MHALF = col(0, 2), col(2), col(3)
        BIAS1 = [col(4), col(5)]
        BIAS2 = [col(6), col(7)]
        GM = [col(8), col(9)]
        Z1, Z2, Z3, SC, NEGM = col(10), col(11), col(12), col(34), col(35)
        RSUM, NONE, DEN, RINV = col(13), col(14), col(15), col(16)
        STATS, MV, VE, RSTD = col(17, 6), col(23, 2), col(25), col(26)
        LD, LG = col(27), col(28)
        PAD = col(29)
        DMX = col(30, 4)

        x_all = wh
        strict = E[:, 0, 0:P]
        WX = D + 2
        w_sb = E[:, 1, 0:KD * WX].rearrange("p (k d) -> p k d", k=KD)
        a_row = E[:, 2, 0:2 * D].rearrange("p (k d) -> p k d", k=2)
        ones = E[:, 3, 0:P]
        stat_all = nb[:, 0, 0:16 * L].bitcast(F32)
        mv_all = nb[:, 0, 16 * L:20 * L].bitcast(F32)
        rstd_all = nb[:, 0, 20 * L:22 * L].bitcast(F32)
        half_all = nb[:, 0, 22 * L:24 * L].bitcast(F32)
        hn = adj_sb[:, :, 0:D]
        hnT = adj_sb[:, :, D:2 * D].rearrange("p u (k q) -> p u k q", k=KD)
        dump = adj_sb[:, :, 2 * D:3 * D]
        part_sum = adj_sb[:, 0, 3 * D:4 * D]
        BACK = 4
        back = [nb[:, s // 2, s % 2 * (N // 2):s % 2 * (N // 2) + 2 * (G4 + D)].bitcast(F32) for s in range(BACK)]
        xp_slot, x1_slot = [b[:, 0:G4] for b in back], [b[:, G4:G4 + D] for b in back]
        xp_again, x1_again = xp_slot[0], x1_slot[0]
        st_cols = base[:, 0:2 * L].rearrange("p (a b) -> p a b", a=2)
        st_out = w1[:, :].rearrange("p (a b) -> p a b", a=2)

        XL = 8
        XB = L // XL
        x_loaded = [sem(f"x_loaded{i}") for i in range(XL)]
        w_loaded, row_loaded = sem("w_loaded"), sem("row_loaded")
        consts = sem("consts")
        st_done, ag_done = sem("st_done"), sem("ag_done")
        rs_done, rs_in = sem("rs_done"), sem("rs_in")
        hn_ready, hnT_mm, hnT_ready = sem("hn_ready"), sem("hnT_mm"), sem("hnT_ready")
        wh_mm, wh_ready, st_ready = sem("wh_mm"), sem("wh_ready"), sem("st_ready")
        cs_mm, stT_mm, stT_ready = sem("cs_mm"), sem("stT_mm"), sem("stT_ready")
        line_stored, line_loaded = sem("line_stored"), sem("line_loaded")
        prep, tmin_ready = sem("prep"), sem("tmin_ready")
        adj_loaded = [sem("adj_loaded0"), sem("adj_loaded1")]
        held = sem("held")
        prep2, bias_sum = sem("prep2"), sem("bias_sum")
        wa_ready, tmin_mm, part_ready = sem("wa_ready"), sem("tmin_mm"), sem("part_ready")

        with nc.Block() as block:
            @block.sync
            def _(sp):
                for i in range(XL):
                    sp.dma_start(x_all[:, i * XB:(i + 1) * XB, :],
                                 x[i * XB * P:(i + 1) * XB * P, :].rearrange("(b p) d -> p b d", p=P)
                                 ).then_inc(x_loaded[i], 16)
                sp.wait_ge(stT_ready, 1)
                for i, line in enumerate((s_line, t_line)):
                    sp.dma_start(line.rearrange("(b p) -> b p", p=P), st_out[0:L, i, :]).then_inc(line_stored, 16)
                sp.wait_ge(line_stored, 32)
                sp.dma_start(t_row[:, :], t_line.rearrange("(o n) -> o n", o=1).to_broadcast([P, N])).then_inc(line_loaded, 16)
                s_kl = s_line.rearrange("(k l) -> k l", l=L)
                sp.dma_start(s_perm[:, 0:WARM], s_kl[:, OFF:L]).then_inc(line_loaded, 16)
                sp.dma_start(s_perm[:, WARM:L], s_kl[:, 0:OFF]).then_inc(line_loaded, 16)
                sp.wait_ge(cs_mm, 1)
                for c in range(2):
                    sp.dma_start(adj_sb[:, c, :], adj_kl[:, OFF, c * CHUNK:(c + 1) * CHUNK]).then_inc(adj_loaded[c], 16)
                sp.wait_ge(line_loaded, 48)

            @block.scalar
            def _(act):
                act.dma_start(w_sb[:, :, 0:D], w_gnn.rearrange("(k p) d -> p k d", p=P)).then_inc(w_loaded, 16)
                act.dma_start(a_row, a_pair.rearrange("(o a d) c -> o a (d c)", o=1, a=2).to_broadcast([P, 2, D])).then_inc(w_loaded, 16)
                act.dma_start(wih[:, :, :], w_ih_t.rearrange("(k p) g -> p k g", p=P)).then_inc(row_loaded, 16)
                act.dma_start(whh[:, :, :], w_hh_t.rearrange("(k p) g -> p k g", p=P)).then_inc(row_loaded, 16)
                act.dma_start(bias[:, :], b_ih.rearrange("(o g) -> o g", o=1).to_broadcast([P, G4])).then_inc(row_loaded, 16)
                act.dma_start(xp[:, :], b_hh.rearrange("(o g) -> o g", o=1).to_broadcast([P, G4])).then_inc(row_loaded, 16)
                act.dma_start(fb[:, 0, :], fw.to_broadcast([P, D])).then_inc(row_loaded, 16)
                act.dma_start(fb[:, 1, :], bw.to_broadcast([P, D])).then_inc(row_loaded, 16)
                act.dma_start(BL, b_lin.rearrange("(o g) -> o g", o=1).to_broadcast([P, 2])).then_inc(row_loaded, 16)
                act.dma_start(wl[:, :, :], w_lin_t.rearrange("(k p) g -> p k g", p=P)).then_inc(row_loaded, 16)
                act.wait_ge(consts, 5)
                nc.scalar.activation(Z3, MHALF, ACT.Tanh)

                def collect(b, u):
                    act.wait_ge(hnT_mm, b + 1)
                    nc.scalar.copy(hnT[:, u, :, :].rearrange("p k q -> p (k q)"), ps_t[u][:, 0:D]).then_inc(hnT_ready, 1)

                def take(b, u):
                    act.wait_ge(wh_mm, b + 1)
                    hold(act)
                    nc.scalar.copy(wh[:, bass.ds(b, 1), :].rearrange("p o d -> p (o d)"), ps_o[u][:, 0:D]).then_inc(wh_ready, 1)
                    nc.scalar.copy(st_cols[:, :, bass.ds(b, 1)].rearrange("p a o -> p (a o)"), ps_o[u][:, D:WX]).then_inc(st_ready, 1)

                collect(0, 0)
                collect(1, 1)
                take(0, 0)
                with act.Fori(0, L // 2 - 1) as i:
                    for u in range(2):
                        collect(2 * i + (2 + u), u)
                        take(2 * i + (1 + u), 1 - u)
                take(L - 1, 1)

            @block.gpsimd
            def _(pool):
                nc.gpsimd.memset(ones, 1.0).then_inc(consts, 1)
                nc.gpsimd.memset(ident[:, :], 1.0).then_inc(consts, 1)
                nc.gpsimd.memset(MHALF, -0.5).then_inc(consts, 1)
                nc.gpsimd.memset(half_all, -0.5).then_inc(consts, 1)
                pool.wait_ge(consts, 4)
                nc.gpsimd.affine_select(out=ident[:, :], in_=ident[:, :], compare_op=ALU.is_equal, fill=0.0,
                                        base=0, pattern=[[-1, P]], channel_multiplier=1).then_inc(consts, 1)

                def rstd(g):
                    pool.wait_ge(rs_in, g + 1)
                    part = rstd_all[:, g * XB:(g + 1) * XB]
                    nc.gpsimd.tensor_tensor(part, part, half_all[:, g * XB:(g + 1) * XB], ALU.pow).then_inc(rs_done, 1)

                nc.gpsimd.memset(part_sum, 0.0).then_inc(part_ready, 1)
                rstd(0)
                rstd(1)
                for g in range(XL):
                    if g + 2 < XL:
                        rstd(g + 2)
                    with pool.Fori(g * XB, (g + 1) * XB) as b:
                        pool.wait_ge(wh_ready, b + 1)
                        hold(pool)
                        pool.wait_ge(part_ready, b + 1)
                        hold(pool)
                        nc.gpsimd.tensor_tensor(part_sum, part_sum, wh[:, bass.ds(b, 1), :].rearrange("p o d -> p (o d)"),
                                                ALU.add).then_inc(part_ready, 1)

            @block.vector
            def _(dve):
                def stats(g):
                    blocks = range(g * XB, (g + 1) * XB)
                    dve.wait_ge(x_loaded[g], 16)
                    for b in blocks:
                        nc.vector.bn_stats(stat_all[:, 6 * b:6 * b + 6], x_all[:, b, :]).then_inc(st_done, 1)
                    for b in blocks:
                        dve.wait_ge(st_done, b + 1)
                        nc.vector.bn_aggr(mv_all[:, 2 * b:2 * b + 2], stat_all[:, 6 * b:6 * b + 6]).then_inc(ag_done, 1)
                    dve.wait_ge(ag_done, (g + 1) * XB)
                    nc.vector.tensor_scalar(rstd_all[:, g * XB:(g + 1) * XB],
                                            mv_all.rearrange("p (b c) -> p b c", c=2)[:, g * XB:(g + 1) * XB, 1],
                                            EPS, None, ALU.add).then_inc(rs_in, 1)

                stats(0)
                dve.wait_ge(w_loaded, 32)
                for k in range(KD):
                    for h in range(2):
                        nc.vector.scalar_tensor_tensor(out=dump[:, h, :], in0=w_sb[:, k, 0:D], scalar=1.0, in1=a_row[:, h, :], op0=ALU.mult,
                                                       op1=ALU.mult, accum_out=w_sb[:, k, D + h:D + h + 1]).then_inc(wa_ready, 1)
                        dve.wait_ge(wa_ready, 2 * k + h + 1)

                def norm(b, u):
                    nc.vector.tensor_scalar(hn[:, u, :], x_all[:, bass.ds(b, 1), :].rearrange("p o d -> p (o d)"),
                                            mv_all[:, bass.ds(2 * b, 1)], rstd_all[:, bass.ds(b, 1)],
                                            ALU.subtract, ALU.mult).then_inc(hn_ready, 1)

                def norm_ahead(b, u):
                    dve.wait_ge(hnT_mm, b + 1)
                    hold(dve)
                    norm(b + 2, u)

                dve.wait_ge(rs_done, 1)
                norm(0, 0)
                norm(1, 1)
                stats(1)
                for g in range(XL):
                    if g + 2 < XL:
                        stats(g + 2)
                    if g + 1 < XL:
                        dve.wait_ge(rs_done, g + 2)
                    with dve.Fori(g * XB // 2, ((g + 1) * XB - (2 if g == XL - 1 else 0)) // 2) as i:
                        for u in range(2):
                            norm_ahead(2 * i + u, u)
                dve.wait_ge(st_ready, L)
                nc.vector.tensor_reduce(out=Z1, in_=st_cols[:, 1, :], axis=AX.X, op=ALU.min).then_inc(tmin_ready, 1)
                dve.wait_ge(tmin_mm, 1)
                nc.vector.tensor_reduce(out=TMIN[0:1, :], in_=ps_x[0:1, 0:P], axis=AX.X, op=ALU.min).then_inc(tmin_ready, 1)
                dve.wait_ge(tmin_mm, 2)
                nc.vector.tensor_copy(Z2, ps_x[:, P:P + 1]).then_inc(tmin_ready, 1)
                dve.wait_ge(tmin_ready, 3)
                nc.vector.tensor_scalar(st_cols[:, 1, :], st_cols[:, 1, :], Z2, 1.0, ALU.subtract, ALU.add)
                nc.vector.tensor_scalar(st_cols[:, 0, :], st_cols[:, 0, :], Z2, -1.0, ALU.add, ALU.add).then_inc(prep2, 1)
                dve.wait_ge(stT_mm, 1)
                nc.vector.tensor_copy(st_out[0:L, :, :], ps_h[0:L, 0:2 * P].rearrange("p (a b) -> p a b", a=2)).then_inc(stT_ready, 1)
                dve.wait_ge(row_loaded, 8 * 16)
                for t, scale in ((wih, 1.0), (whh, 0.5)):
                    for lo, hi, f in ((0, 2 * D, 0.5), (2 * D, 3 * D, 1.0), (3 * D, G4, 0.5)):
                        if scale * f != 1.0:
                            nc.vector.tensor_scalar(t[:, :, lo:hi], t[:, :, lo:hi], scale * f, None, ALU.mult)
                nc.vector.tensor_scalar(wl[:, :, :], wl[:, :, :], 0.5, None, ALU.mult)
                nc.vector.tensor_scalar(fb[:, :, :], fb[:, :, :], 0.5, None, ALU.mult)
                nc.vector.tensor_tensor(bias[:, :], bias[:, :], xp[:, :], ALU.add).then_inc(bias_sum, 1)
                dve.wait_ge(bias_sum, 1)
                nc.vector.tensor_scalar(bias[:, 0:2 * D], bias[:, 0:2 * D], 0.5, None, ALU.mult)
                nc.vector.tensor_scalar(bias[:, 3 * D:G4], bias[:, 3 * D:G4], 0.5, None, ALU.mult)
                nc.vector.memset(hT[:, :, :], 0.0)
                nc.vector.memset(c2[:, :], 0.0)
                nc.vector.memset(S2[:, :, :], 0.0)
                dve.wait_ge(cs_mm, 1)
                nc.vector.tensor_copy(csum[:, :], ps_g[0][:, 0:D])

            @block.tensor
            def _(pe):
                pe.wait_ge(consts, 5)
                pe.wait_ge(w_loaded, 32)

                def turn(b, u):
                    pe.wait_ge(hn_ready, b + 1)
                    for k in range(KD):
                        last = nc.tensor.transpose(ps_t[u][:, k * P:(k + 1) * P], hn[:, u, k * P:(k + 1) * P], ident[:, :])
                    last.then_inc(hnT_mm, 1)

                def product(b, u):
                    pe.wait_ge(hnT_ready, b + 1)
                    if not isinstance(b, int) or b >= 2:
                        pe.wait_ge(st_ready, b - 1)
                    for k in range(KD):
                        last = nc.tensor.matmul(ps_o[u][:, 0:WX], hnT[:, u, k, :], w_sb[:, k, :], start=k == 0, stop=k == KD - 1)
                    last.then_inc(wh_mm, 1)

                pe.wait_ge(wa_ready, 2 * KD)
                turn(0, 0)
                turn(1, 1)
                product(0, 0)
                turn(2, 0)
                product(1, 1)
                turn(3, 1)
                product(2, 0)
                with pe.Fori(0, L // 2 - 2) as i:
                    for u in range(2):
                        turn(2 * i + (4 + u), u)
                        product(2 * i + (3 + u), 1 - u)
                product(L - 1, 1)
                pe.wait_ge(tmin_ready, 1)
                nc.tensor.matmul(ps_x[0:1, 0:P], Z1, ident[:, :], start=True, stop=True).then_inc(tmin_mm, 1)
                pe.wait_ge(tmin_ready, 2)
                nc.tensor.matmul(ps_x[:, P:P + 1], ones[0:1, :], TMIN[0:1, :], start=True, stop=True).then_inc(tmin_mm, 1)
                pe.wait_ge(prep2, 1)
                for k in range(2):
                    last = nc.tensor.transpose(ps_h[0:L, k * P:(k + 1) * P], st_cols[:, k, :], ident[:, :])
                last.then_inc(stT_mm, 1)
                pe.wait_ge(part_ready, L + 1)
                nc.tensor.matmul(ps_g[0][:, 0:D], ones, part_sum, start=True, stop=True).then_inc(cs_mm, 1)


        xi_loaded = [sem("xi_loaded0"), sem("xi_loaded1")]
        guard_done, guard_max = sem("guard_done"), sem("guard_max")
        y_ready, y_sum, e_ready, p_ready = sem("y_ready"), sem("y_sum"), sem("e_ready"), sem("p_ready")
        turned, pt_ready, acc_ready = sem("turned"), sem("pt_ready"), sem("acc_ready")
        fin, elu_ready, rstd_ready, x1_stored = sem("fin"), sem("elu_ready"), sem("rstd_ready"), sem("x1_stored")
        xnT_mm, xnT_ready = sem("xnT_mm"), sem("xnT_ready")
        in_mm, in_ready, in_stored = sem("in_mm"), sem("in_ready"), sem("in_stored")
        rec_mm, gate_sum, gate_act = sem("rec_mm"), sem("gate_sum"), sem("gate_act")
        cell, cell_act, h_ready = sem("cell"), sem("cell_act"), sem("h_ready")
        hT_mm, hT_ready = sem("hT_mm"), sem("hT_ready")
        logit_mm, picked = sem("logit_mm"), sem("picked")
        part_a, base_ready, base_stored = sem("part_a"), sem("base_ready"), sem("base_stored")
        shift_mm, shifted, shifted_h = sem("shift_mm"), sem("shifted"), sem("shifted_h")
        shift_made, end_stored = sem("shift_made"), sem("end_stored")
        x1_free, x1_added = sem("x1_free"), sem("x1_added")
        xp_back = [sem(f"xp_back{s}") for s in range(BACK)]
        x1_back = [sem(f"x1_back{s}") for s in range(BACK)]
        FIN = 16
        LEAD = 3

        def at(n, per, k):
            return n * per + k

        def tiles(eng, body):
            body(0, 0, True, None, 0)
            with eng.Fori(0, WARM // 2) as i:
                for u in range(2):
                    body(2 * i + 1 + u, (1 + u) % 2, True, "warm", 0)
            yield
            body(WARM + 1, 1, True, "main", 0)
            body(WARM + 2, 0, True, "main", 1)
            with eng.Fori(0, (L - 4 - WARM) // 2) as i:
                for u in range(2):
                    body(2 * i + WARM + 3 + u, (1 + u) % 2, True, "main", 2)
            body(L - 1, 1, False, "main", 2)

        with nc.Block() as block:
            @block.sync
            def _(sp):
                def load(n, position, u, first=False):
                    for c in range(2 if first else 0, NCH):
                        sp.wait_ge(guard_done, at(n, NCH, c - 1))
                        sp.dma_start(adj_sb[:, c % 2, :],
                                     adj_kl[:, bass.ds(position, 1), c * CHUNK:(c + 1) * CHUNK].rearrange("k o j -> k (o j)")
                                     ).then_inc(adj_loaded[c % 2], 16)
                    if not first:
                        sp.wait_ge(fin, FIN * n - (2 * FIN - 8))
                    sp.dma_start(x_in[:, u, :], x_kl[:, bass.ds(position, 1), :].rearrange("k o d -> k (o d)")).then_inc(xi_loaded[u], 16)

                load(0, OFF, 0, True)
                for c in range(NCH):
                    sp.wait_ge(guard_done, NCH + c - 1)
                    sp.dma_start(adj_sb[:, c % 2, :], adj_kl[:, OFF + 1, c * CHUNK:(c + 1) * CHUNK]).then_inc(adj_loaded[c % 2], 16)
                sp.dma_start(x_in[:, 1, :], x_kl[:, OFF + 1, :]).then_inc(xi_loaded[1], 16)
                with sp.Fori(0, WARM // 2 - 1) as i:
                    for u in range(2):
                        load(2 * i + 2 + u, 2 * i + (OFF + 2 + u), u)
                with sp.Fori(0, (L - WARM) // 2) as i:
                    for u in range(2):
                        load(2 * i + WARM + u, 2 * i + u, u)
                sp.wait_ge(p_ready, NP * L)
                sp.wait_ge(in_stored, 16 * (L - 2))
                sp.wait_ge(x1_stored, 16 * (L - 2))
                for s in range(BACK):
                    sp.dma_start(xp_slot[s], xp_dram[:, OFF + s, :]).then_inc(xp_back[s], 16)
                    sp.dma_start(x1_slot[s], x1_dram[:, OFF + s, :]).then_inc(x1_back[s], 16)

            @block.gpsimd
            def _(pool):
                pool.sem_inc(x1_free, 1)
                pool.sem_inc(x1_added, 1)
                pool.sem_inc(base_ready, 1)
                pool.sem_inc(gate_sum, 2)
                pool.sem_inc(hT_ready, 1)
                pool.sem_inc(picked, 3)
                nc.gpsimd.memset(shift[:, :], 1.0).then_inc(shift_made, 1)
                pool.wait_ge(shift_made, 1)
                nc.gpsimd.affine_select(out=shift[:, :], in_=shift[:, :], compare_op=ALU.is_equal, fill=0.0,
                                        base=1, pattern=[[-1, P]], channel_multiplier=1).then_inc(shift_made, 1)

                def finish_x(m, position):
                    pool.wait_ge(fin, at(m, FIN, 12))
                    hold(pool)
                    pool.dma_start(x1_dram[:, bass.ds(position, 1), :].rearrange("k o d -> k (o d)"), x1[:, :]).then_inc(x1_stored, 16)

                def finish_rstd(m):
                    pool.wait_ge(fin, at(m, FIN, 15))
                    nc.gpsimd.tensor_tensor(RSTD, VE, MHALF, ALU.pow).then_inc(rstd_ready, 1)

                def finish_in(m, position):
                    pool.wait_ge(x1_stored, at(m, 16, 16))
                    pool.sem_inc(x1_free, 1)
                    pool.wait_ge(in_ready, at(m, 2, 2))
                    hold(pool)
                    pool.dma_start(xp_dram[:, bass.ds(position, 1), :].rearrange("k o g -> k (o g)"), xp[:, :]).then_inc(in_stored, 16)

                def forward_part(mm, u, x1=x1[:, :]):
                    if not (isinstance(mm, int) and mm == 0):
                        pool.wait_ge(base_stored, at(mm, 16, 0))
                    pool.wait_ge(picked, at(mm, 3, 6))
                    nc.gpsimd.tensor_tensor(base[:, :], x1, h2[:, :], ALU.add).then_inc(x1_added, 1)
                    nc.gpsimd.tensor_tensor(w3[:, :], S2[:, u, :], fb[:, 0, :], ALU.mult).then_inc(part_a, 1)
                    pool.wait_ge(x1_added, at(mm, 1, 2))
                    hold(pool)
                    pool.wait_ge(part_a, at(mm, 3, 1))
                    nc.gpsimd.tensor_tensor(base[:, :], base[:, :], w3[:, :], ALU.add).then_inc(part_a, 1)

                def backward_part(mm, u):
                    pool.wait_ge(part_a, at(mm, 3, 2))
                    nc.gpsimd.tensor_tensor(w3[:, :], S2[:, 1 - u, :], fb[:, 1, :], ALU.mult).then_inc(part_a, 1)
                    pool.wait_ge(part_a, at(mm, 3, 3))
                    nc.gpsimd.tensor_tensor(base[:, :], base[:, :], w3[:, :], ALU.subtract).then_inc(base_ready, 1)

                def store_base(mm, position):
                    pool.wait_ge(base_ready, at(mm, 1, 2))
                    hold(pool)
                    pool.dma_start(base_dram[:, bass.ds(position, 1), :].rearrange("k o d -> k (o d)"), base[:, :]).then_inc(base_stored, 16)

                def output(mm, u, position, x1=x1[:, :]):
                    forward_part(mm, u, x1)
                    backward_part(mm, u)
                    store_base(mm, position)

                def scores(n, p):
                    pool.wait_ge(y_ready, at(n, NP, p + 1))
                    slot = E[:, p % E_SLOTS, :]
                    nc.gpsimd.tensor_tensor(slot, slot, t_row[:, p * PIECE:(p + 1) * PIECE], ALU.add).then_inc(y_sum, 1)

                when = {0: (3,), 1: (4,), 2: (1,), 3: (0, 5), 5: (2,)}

                def turn(n, u, more, prev, late):
                    for p in range(NP):
                        q = p + LEAD
                        if q < NP:
                            scores(n, q)
                        elif more:
                            scores(n + 1, q - NP)
                        if prev:
                            m, v = n - 1, 1 - u
                            mm = m - WARM if prev == "main" else None
                            position = m - WARM if prev == "main" else m + OFF
                            for k in when.get(p, ()):
                                if k == 0:
                                    finish_x(m, position)
                                elif k == 1:
                                    finish_rstd(m)
                                elif k == 2:
                                    finish_in(m, position)
                                elif late and k == 3:
                                    forward_part(mm - 1, u)
                                elif late and k == 4:
                                    backward_part(mm - 1, u)
                                elif late and k == 5:
                                    store_base(mm - 1, position - 1)

                for p in range(LEAD):
                    scores(0, p)
                for _ in tiles(pool, turn):
                    pass
                output(L - 2 - WARM, 0, OFF - 2)
                finish_x(L - 1, OFF - 1)
                finish_rstd(L - 1)
                finish_in(L - 1, OFF - 1)
                output(L - 1 - WARM, 1, OFF - 1)
                pool.wait_ge(base_stored, 16 * OFF)
                pool.wait_ge(x1_stored, 16 * L)
                pool.wait_ge(in_stored, 16 * L)

            @block.scalar
            def _(act):
                def scores(n, u, p):
                    if p == 0:
                        act.wait_ge(guard_max, at(n, 6, 6))
                    if not (isinstance(n, int) and n == 0 and p < E_SLOTS):
                        act.wait_ge(turned, at(n, NG, GPP * (p - E_SLOTS + 1)))
                    nc.scalar.activation(E[:, p % E_SLOTS, :], t_row[:, p * PIECE:(p + 1) * PIECE], ACT.Relu,
                                         bias=BIAS1[u], scale=1.0 / SLOPE - 1.0).then_inc(y_ready, 1)

                def exponentials(n, u, p):
                    act.wait_ge(y_sum, at(n, NP, p + 1))
                    slot = E[:, p % E_SLOTS, :]
                    nc.scalar.activation(slot, slot, ACT.Exp, bias=BIAS2[u], scale=SLOPE).then_inc(e_ready, 1)

                def collect(n, g):
                    act.wait_ge(turned, at(n, NG, g + 1))
                    nc.scalar.copy(PT[:, g % 2, :], ps_t[g % 2][:, :]).then_inc(pt_ready, 1)

                def gates(m, xp=xp[:, :]):
                    act.wait_ge(gate_sum, at(m, 2, 4))
                    nc.scalar.activation(xp, xp, ACT.Tanh).then_inc(gate_act, 1)

                def cell_out(m):
                    act.wait_ge(cell, at(m, 3, 3))
                    nc.scalar.activation(w1[:, :], c2[:, :], ACT.Tanh, scale=0.5).then_inc(cell_act, 1)

                def state_turned(m):
                    act.wait_ge(hT_mm, at(m, 1, 1))
                    nc.scalar.copy(hT[:, :, :].rearrange("p k q -> p (k q)"), ps_h[:, 0:D]).then_inc(hT_ready, 1)

                when = {2: 0, 6: 1, 12: 2, 13: 3, 14: 4}

                def turn(n, u, more, prev, late):
                    for g in range(NG):
                        part, p = (scores, exponentials)[g % GPP], g // GPP + LEAD
                        if g % GPP == 1:
                            collect(n, g)
                        if p < NP:
                            part(n, u, p)
                        elif more:
                            part(n + 1, 1 - u, p - NP)
                        if g % GPP == 0:
                            collect(n, g)
                        if prev:
                            for h, k in when.items():
                                if h == g:
                                    m, v = n - 1, 1 - u
                                    if k == 0:
                                        act.wait_ge(fin, at(m, FIN, 7))
                                        nc.scalar.activation(w2[:, :], w2[:, :], ACT.Tanh, scale=0.5).then_inc(elu_ready, 1)
                                    elif k == 1:
                                        act.wait_ge(xnT_mm, at(m, 1, 1))
                                        nc.scalar.copy(xnT[:, :, :].rearrange("p k q -> p (k q)"), ps_x[:, 0:D]).then_inc(xnT_ready, 1)
                                    elif k == 2:
                                        gates(m)
                                    elif k == 3:
                                        cell_out(m)
                                    else:
                                        state_turned(m)

                for p in range(LEAD):
                    scores(0, 0, p)
                for p in range(LEAD):
                    exponentials(0, 0, p)
                for _ in tiles(act, turn):
                    act.wait_ge(h_ready, WARM)
                    act.dma_start(end_dram[0], h2[:, :]).then_inc(end_stored, 16)
                    act.dma_start(end_dram[1], c2[:, :]).then_inc(end_stored, 16)
                    act.wait_ge(shift_mm, 1)
                    nc.scalar.copy(hT[:, :, :].rearrange("p k q -> p (k q)"), ps_h[:, 0:D]).then_inc(shifted_h, 1)
                m = L - 1
                act.wait_ge(fin, at(m, FIN, 7))
                nc.scalar.activation(w2[:, :], w2[:, :], ACT.Tanh, scale=0.5).then_inc(elu_ready, 1)
                act.wait_ge(xnT_mm, m + 1)
                nc.scalar.copy(xnT[:, :, :].rearrange("p k q -> p (k q)"), ps_x[:, 0:D]).then_inc(xnT_ready, 1)

                def step(m, xp=xp[:, :]):
                    gates(m, xp)
                    cell_out(m)
                    state_turned(m)
                step(L - 1)

            @block.vector
            def _(dve):
                def guard(n, u, c):
                    dve.wait_ge(adj_loaded[c % 2], at(n, 16 * NCH // 2, 16 * (c // 2) + 16))
                    hold(dve)
                    nc.vector.tensor_tensor_reduce(out=nb[:, u, c * CHUNK:(c + 1) * CHUNK], in0=adj_sb[:, c % 2, :],
                                                   in1=t_row[:, c * CHUNK:(c + 1) * CHUNK], scale=1.0, scalar=0.0,
                                                   op0=ALU.mult, op1=ALU.max, accum_out=gmx[:, u, c:c + 1]).then_inc(guard_done, 1)

                def row_max(n, u):
                    dve.wait_ge(guard_done, at(n, NCH, NCH))
                    nc.vector.tensor_reduce(out=GM[u], in_=gmx[:, u, :], axis=AX.X, op=ALU.max).then_inc(guard_max, 1)
                    nc.vector.tensor_copy(SC, s_perm[:, bass.ds(n, 1)]).then_inc(guard_max, 1)
                    dve.wait_ge(guard_max, at(n, 6, 2))
                    nc.vector.tensor_tensor(Z1, GM[u], SC, ALU.add).then_inc(guard_max, 1)
                    dve.wait_ge(guard_max, at(n, 6, 3))
                    nc.vector.tensor_scalar(Z2, Z1, -SLOPE, -1.0, ALU.mult, ALU.add)
                    nc.vector.tensor_scalar(Z3, Z1, -1.0, -1.0, ALU.mult, ALU.add).then_inc(guard_max, 1)
                    dve.wait_ge(guard_max, at(n, 6, 4))
                    nc.vector.tensor_tensor(NEGM, Z2, Z3, ALU.min).then_inc(guard_max, 1)
                    dve.wait_ge(guard_max, at(n, 6, 5))
                    nc.vector.tensor_scalar(BIAS1[u], SC, 1.0 / SLOPE - 1.0, None, ALU.mult)
                    nc.vector.scalar_tensor_tensor(out=BIAS2[u], in0=SC, scalar=SLOPE, in1=NEGM, op0=ALU.mult,
                                                   op1=ALU.add).then_inc(guard_max, 1)

                def weights(n, u, p):
                    e = E[:, p % E_SLOTS, :]
                    dve.wait_ge(e_ready, at(n, NP, p + 1))
                    nc.vector.scalar_tensor_tensor(out=e, in0=nb[:, u, p * PIECE:(p + 1) * PIECE], scalar=0.0, in1=e,
                                                   op0=ALU.is_gt, op1=ALU.min, accum_out=rs[:, u, p:p + 1]).then_inc(p_ready, 1)

                def counted(m, first):
                    k = [first]

                    def step(ins, wait=True):
                        k[0] += 1
                        ins.then_inc(fin, 1)
                        if wait:
                            dve.wait_ge(fin, at(m, FIN, k[0]))
                    return step

                def divide(m, u):
                    step, v = counted(m, 0), nc.vector
                    dve.wait_ge(p_ready, at(m, NP, NP))
                    step(v.tensor_reduce(out=RSUM, in_=rs[:, u, :], axis=AX.X, op=ALU.add), False)
                    step(v.tensor_scalar(NONE, GM[u], 0.0, None, ALU.is_le))
                    step(v.scalar_tensor_tensor(out=DEN, in0=NONE, scalar=float(N), in1=RSUM, op0=ALU.mult, op1=ALU.add))
                    step(v.reciprocal(RINV, DEN), False)
                    dve.wait_ge(acc_ready, at(m, 1, 1))
                    step(v.scalar_tensor_tensor(out=w1b[:, :], in0=csum[:, :], scalar=NONE, in1=ps_o[u][:, 0:D], op0=ALU.mult, op1=ALU.add))
                    step(v.tensor_scalar(w1b[:, :], w1b[:, :], RINV, None, ALU.mult))
                    step(v.tensor_scalar(w2[:, :], w1b[:, :], 0.0, None, ALU.min), False)
                    dve.wait_ge(xi_loaded[u], at(m, 8, 16 - 8 * u))
                    step(v.scalar_tensor_tensor(out=w1b[:, :], in0=w1b[:, :], scalar=0.0, in1=x_in[:, u, :], op0=ALU.max, op1=ALU.add), False)

                def normalise(m, mm):
                    step, v = counted(m, 8), nc.vector
                    dve.wait_ge(elu_ready, at(m, 1, 1))
                    step(v.tensor_scalar(xn[:, :], w2[:, :], -1.0, 1.0, ALU.mult, ALU.add))
                    step(v.reciprocal(xn[:, :], xn[:, :]))
                    step(v.scalar_tensor_tensor(out=w2[:, :], in0=w2[:, :], scalar=2.0, in1=xn[:, :], op0=ALU.mult, op1=ALU.mult))
                    dve.wait_ge(x1_free, at(m, 1, 1))
                    if mm is not None:
                        dve.wait_ge(x1_added, at(mm, 1, 1))
                    step(v.tensor_tensor(x1[:, :], w1b[:, :], w2[:, :], ALU.add))
                    step(v.bn_stats(STATS, x1[:, :]))
                    hold(dve)
                    step(v.bn_aggr(MV, STATS))
                    step(v.tensor_scalar(VE, MV[:, 1:2], EPS, None, ALU.add), False)

                def normalised(m):
                    step, v = counted(m, 15), nc.vector
                    dve.wait_ge(rstd_ready, at(m, 1, 1))
                    step(v.tensor_scalar(xn[:, :], x1[:, :], MV[:, 0:1], RSTD, ALU.subtract, ALU.mult), False)

                def inputs(m):
                    for h in range(2):
                        dve.wait_ge(in_mm, at(m, 2, h + 1))
                        nc.vector.tensor_tensor(xp[:, h * HALF:(h + 1) * HALF], ps_g[h][:, :], bias[:, h * HALF:(h + 1) * HALF],
                                                ALU.add).then_inc(in_ready, 1)

                def gates(m, xp=xp, stored=True):
                    if stored:
                        dve.wait_ge(in_stored, at(m, 16, 16))
                    for h in range(2):
                        dve.wait_ge(rec_mm, at(m, 2, h + 1))
                        half = xp[:, h * HALF:(h + 1) * HALF]
                        nc.vector.tensor_tensor(half, half, ps_g[h][:, :], ALU.add).then_inc(gate_sum, 1)

                def new_cell(m, xp=xp):
                    dve.wait_ge(gate_act, at(m, 1, 1))
                    nc.vector.scalar_tensor_tensor(out=w1b[:, :], in0=xp[:, D:2 * D], scalar=1.0, in1=c2[:, :],
                                                   op0=ALU.add, op1=ALU.mult).then_inc(cell, 1)
                    nc.vector.scalar_tensor_tensor(out=xn[:, :], in0=xp[:, 0:D], scalar=1.0, in1=xp[:, 2 * D:3 * D],
                                                   op0=ALU.add, op1=ALU.mult).then_inc(cell, 1)
                    dve.wait_ge(cell, at(m, 3, 2))
                    nc.vector.scalar_tensor_tensor(out=c2[:, :], in0=w1b[:, :], scalar=0.5, in1=xn[:, :],
                                                   op0=ALU.mult, op1=ALU.add).then_inc(cell, 1)

                def new_state(m, mm, xp=xp):
                    if mm is not None:
                        dve.wait_ge(base_ready, at(mm, 1, 1))
                    dve.wait_ge(cell_act, at(m, 1, 1))
                    nc.vector.scalar_tensor_tensor(out=h2[:, :], in0=xp[:, 3 * D:G4], scalar=1.0, in1=w1[:, :],
                                                   op0=ALU.add, op1=ALU.mult).then_inc(h_ready, 1)

                def pick(mm, u):
                    dve.wait_ge(logit_mm, at(mm, 1, 1))
                    nc.vector.tensor_scalar(LD, ps_h[:, 0:1], BL[:, 0:1], None, ALU.add).then_inc(picked, 1)
                    dve.wait_ge(picked, at(mm, 3, 4))
                    nc.vector.tensor_scalar(LG, ps_h[:, 1:2], BL[:, 1:2], LD, ALU.add, ALU.is_gt).then_inc(picked, 1)
                    dve.wait_ge(picked, at(mm, 3, 5))
                    nc.vector.scalar_tensor_tensor(out=S2[:, 1 - u, :], in0=h2[:, :], scalar=LG, in1=S2[:, u, :],
                                                   op0=ALU.mult, op1=ALU.add).then_inc(picked, 1)

                guard_at = (0, 1, 3, 4)
                when = {1: (0,), 2: (1,), 3: (6,), 5: (2,), 7: (3, 4)}

                def turn(n, u, more, prev, late):
                    for p in range(NP):
                        weights(n, u, p)
                        if prev:
                            m, v = n - 1, 1 - u
                            mm = m - WARM if prev == "main" else None
                            for k in when.get(p, ()):
                                if k == 0:
                                    divide(m, v)
                                elif k == 1:
                                    normalise(m, mm)
                                elif k == 6:
                                    normalised(m)
                                elif k == 2:
                                    inputs(m)
                                elif k == 3:
                                    gates(m)
                                elif k == 4:
                                    new_cell(m)
                                    new_state(m, mm)
                        if more and p in guard_at:
                            guard(n + 1, 1 - u, guard_at.index(p))
                        if late and p == 0:
                            pick(n - 1 - WARM - 1, u)
                        if more and p == 5:
                            row_max(n + 1, 1 - u)

                for c in range(NCH):
                    guard(0, 0, c)
                row_max(0, 0)
                for _ in tiles(dve, turn):
                    dve.wait_ge(end_stored, 32)
                    dve.wait_ge(shift_mm, 1)
                    nc.vector.tensor_copy(c2[:, :], ps_x[:, D:2 * D]).then_inc(shifted, 1)
                pick(L - 2 - WARM, 0)
                divide(L - 1, 1)
                normalise(L - 1, L - 1 - WARM)
                normalised(L - 1)
                inputs(L - 1)
                gates(L - 1)
                new_cell(L - 1)
                new_state(L - 1, L - 1 - WARM)
                pick(L - 1 - WARM, 1)

            @block.tensor
            def _(pe):
                def turned_group(n, g):
                    if g % GPP == 0:
                        pe.wait_ge(p_ready, at(n, NP, g // GPP + 1))
                    p, first = g // GPP, g % GPP * GROUP
                    for b in range(BPG):
                        last = nc.tensor.transpose(ps_t[g % 2][:, b * P:(b + 1) * P],
                                                   E[:, p % E_SLOTS, first + b * P:first + (b + 1) * P], ident[:, :])
                    last.then_inc(turned, 1)

                def summed_group(n, u, g):
                    pe.wait_ge(pt_ready, at(n, NG, g + 1))
                    for b in range(BPG):
                        last = nc.tensor.matmul(ps_o[u][:, 0:D], PT[:, g % 2, b * P:(b + 1) * P], wh[:, g * BPG + b, :],
                                                start=g == 0 and b == 0, stop=g == NG - 1 and b == BPG - 1)
                    if g == NG - 1:
                        last.then_inc(acc_ready, 1)

                def x_turned(m):
                    pe.wait_ge(fin, at(m, FIN, 16))
                    for k in range(KD):
                        last = nc.tensor.transpose(ps_x[:, k * P:(k + 1) * P], xn[:, k * P:(k + 1) * P], ident[:, :])
                    last.then_inc(xnT_mm, 1)

                def x_product(m):
                    pe.wait_ge(xnT_ready, at(m, 1, 1))
                    pe.wait_ge(gate_sum, at(m, 2, 2))
                    for h in range(2):
                        for k in range(KD):
                            last = nc.tensor.matmul(ps_g[h][:, :], xnT[:, k, :], wih[:, k, h * HALF:(h + 1) * HALF], start=k == 0, stop=k == KD - 1)
                        last.then_inc(in_mm, 1)

                def h_product(m, fresh=True):
                    if fresh:
                        pe.wait_ge(in_ready, at(m, 2, 2))
                    else:
                        pe.wait_ge(gate_sum, at(m, 2, 2))
                    pe.wait_ge(hT_ready, at(m, 1, 1))
                    for h in range(2):
                        for k in range(KD):
                            last = nc.tensor.matmul(ps_g[h][:, :], hT[:, k, :], whh[:, k, h * HALF:(h + 1) * HALF], start=k == 0, stop=k == KD - 1)
                        last.then_inc(rec_mm, 1)

                def h_turned(m, mm):
                    pe.wait_ge(h_ready, at(m, 1, 1))
                    if mm is not None:
                        pe.wait_ge(picked, at(mm, 3, 3))
                    for k in range(KD):
                        last = nc.tensor.transpose(ps_h[:, k * P:(k + 1) * P], h2[:, k * P:(k + 1) * P], ident[:, :])
                    last.then_inc(hT_mm, 1)

                def logits(m, mm):
                    pe.wait_ge(hT_ready, at(m, 1, 2))
                    for k in range(KD):
                        last = nc.tensor.matmul(ps_h[:, 0:2], hT[:, k, :], wl[:, k, :], start=k == 0, stop=k == KD - 1)
                    last.then_inc(logit_mm, 1)

                when = {6: (0,), 7: (1,), 10: (2,), 14: (3,), 15: (4,)}

                def turn(n, u, more, prev, late):
                    for g in range(NG):
                        turned_group(n, g)
                        if g > 0:
                            summed_group(n, u, g - 1)
                        elif prev:
                            summed_group(n - 1, 1 - u, NG - 1)
                        if prev:
                            m, v = n - 1, 1 - u
                            mm = m - WARM if prev == "main" else None
                            for k in when.get(g, ()):
                                if k == 0:
                                    x_turned(m)
                                elif k == 1:
                                    x_product(m)
                                elif k == 2:
                                    h_product(m)
                                elif k == 3:
                                    h_turned(m, mm)
                                elif mm is not None:
                                    logits(m, mm)

                for _ in tiles(pe, turn):
                    pe.wait_ge(shift_made, 2)
                    pe.wait_ge(h_ready, WARM)
                    pe.wait_ge(hT_ready, WARM + 1)
                    for k in range(KD):
                        nc.tensor.matmul(ps_h[:, k * P:(k + 1) * P], h2[:, k * P:(k + 1) * P], shift[:, :], start=True, stop=True)
                    nc.tensor.matmul(ps_x[:, D:2 * D], shift[:, :], c2[:, :], start=True, stop=True).then_inc(shift_mm, 1)
                    pe.wait_ge(shifted, 1)
                    pe.wait_ge(shifted_h, 1)
                summed_group(L - 1, 1, NG - 1)
                x_turned(L - 1)
                x_product(L - 1)
                h_product(L - 1)
                h_turned(L - 1, L - 1 - WARM)
                logits(L - 1, L - 1 - WARM)

        x_part_mm, gates_mm, gates_tanh = sem("x_part_mm"), sem("gates_mm"), sem("gates_tanh")
        last_cell, last_cell_tanh, last_h = sem("last_cell"), sem("last_cell_tanh"), sem("last_h")
        last_hT_mm, last_hT, last_logit = sem("last_hT_mm"), sem("last_hT"), sem("last_logit")
        last_pick, last_part, last_out = sem("last_pick"), sem("last_part"), sem("last_out")
        last_added = sem("last_added")
        bases_back, end_in, tables = sem("bases_back"), sem("end_in"), sem("tables")
        parts = [(0, 2 * D), (2 * D, 3 * D), (3 * D, G4)]
        banks = [ps_g + ps_o[0:1], ps_t + ps_o[1:2]]
        h_slot = [E[:, 2, 0:D], h2[:, :]]
        hT_slot = [xnT, hT]
        PER = OFF // WARM
        assert PER * WARM == OFF and WARM % BACK == 0

        def steps(eng, body):
            body(0, 0, True, False)
            with eng.Fori(0, WARM // BACK - 1) as i:
                for s in range(BACK):
                    body(BACK * i + 1 + s, (1 + s) % BACK, False, False)
            for s in range(1, BACK):
                body(WARM - BACK + s, s, False, s == BACK - 1)

        def loads(r, s):
            return 16 // BACK * r + (16 - 16 // BACK * s)

        with nc.Block() as block:
            @block.sync
            def _(sp):
                def bases(r):
                    sp.dma_start(wh[:, bass.ds(r * PER, PER), :], base_dram[:, bass.ds(r * PER, PER), :]).then_inc(bases_back, 16)

                def load(r, s):
                    sp.wait_ge(x_part_mm, r - (BACK - 1))
                    sp.dma_start(xp_slot[s], xp_dram[:, bass.ds(r + OFF, 1), :].rearrange("k o g -> k (o g)")).then_inc(xp_back[s], 16)
                    sp.wait_ge(last_out, r - (BACK - 2))
                    sp.dma_start(x1_slot[s], x1_dram[:, bass.ds(r + OFF, 1), :].rearrange("k o d -> k (o d)")).then_inc(x1_back[s], 16)
                    bases(r)

                for s in range(BACK):
                    bases(s)
                with sp.Fori(0, WARM // BACK - 1) as i:
                    for s in range(BACK):
                        load(BACK * i + BACK + s, s)
                sp.dma_start(x_in[:, 0, :], end_dram[0]).then_inc(end_in, 16)
                sp.dma_start(x_in[:, 1, :], end_dram[1]).then_inc(end_in, 16)
                sp.wait_ge(bases_back, 16 * WARM)
                sp.wait_ge(end_in, 32)

            @block.tensor
            def _(pe):
                def x_part(r, s):
                    u = s % 2
                    pe.wait_ge(xp_back[s], loads(r, s))
                    if not isinstance(r, int) or r >= 2:
                        pe.wait_ge(gates_tanh, 3 * r - 3)
                    for bank, (lo, hi) in zip(banks[u], parts):
                        last = nc.tensor.matmul(bank[:, 0:hi - lo], ident[:, :], xp_slot[s][:, lo:hi], start=True, stop=False)
                    last.then_inc(x_part_mm, 1)

                def h_part(r, u, first):
                    if not first:
                        pe.wait_ge(last_hT, r)
                    for bank, (lo, hi) in zip(banks[u], parts):
                        for k in range(KD):
                            last = nc.tensor.matmul(bank[:, 0:hi - lo], hT_slot[1 - u][:, k, :], whh[:, k, lo:hi], start=False, stop=k == KD - 1)
                        last.then_inc(gates_mm, 1)

                def logits(r, u):
                    pe.wait_ge(last_pick, 3 * r + 3)
                    for k in range(KD):
                        last = nc.tensor.matmul(ps_x[:, 0:2], hT_slot[u][:, k, :], wl[:, k, :], start=k == 0, stop=k == KD - 1)
                    last.then_inc(last_logit, 1)

                def body(r, s, first, final):
                    u = s % 2
                    h_part(r, u, first)
                    if not final:
                        x_part(r + 1, (s + 1) % BACK)
                    pe.wait_ge(last_h, r + 1)
                    for k in range(KD):
                        last = nc.tensor.transpose(ps_h[:, k * P:(k + 1) * P], h_slot[u][:, k * P:(k + 1) * P], ident[:, :])
                    last.then_inc(last_hT_mm, 1)
                    if not first:
                        logits(r - 1, 1 - u)

                x_part(0, 0)
                steps(pe, body)
                pe.wait_ge(last_hT, WARM)
                logits(WARM - 1, 1)

            @block.scalar
            def _(act):
                def body(r, s, first, final):
                    u = s % 2
                    for j, (lo, hi) in enumerate(parts):
                        act.wait_ge(gates_mm, 3 * r + (j + 1))
                        nc.scalar.activation(xp[:, lo:hi], banks[u][j][:, 0:hi - lo], ACT.Tanh).then_inc(gates_tanh, 1)
                    act.wait_ge(last_cell, 3 * r + 3)
                    nc.scalar.activation(w1[:, :], c2[:, :], ACT.Tanh, scale=0.5).then_inc(last_cell_tanh, 1)
                    act.wait_ge(last_hT_mm, r + 1)
                    nc.scalar.copy(hT_slot[u][:, :, :].rearrange("p k q -> p (k q)"), ps_h[:, 0:D]).then_inc(last_hT, 1)
                steps(act, body)

            @block.vector
            def _(dve):
                v = nc.vector

                def pick(r, u):
                    dve.wait_ge(last_logit, r + 1)
                    v.tensor_scalar(LD, ps_x[:, 0:1], BL[:, 0:1], None, ALU.add).then_inc(last_pick, 1)
                    dve.wait_ge(last_pick, 3 * r + 4)
                    v.tensor_scalar(LG, ps_x[:, 1:2], BL[:, 1:2], LD, ALU.add, ALU.is_gt).then_inc(last_pick, 1)
                    dve.wait_ge(last_pick, 3 * r + 5)
                    v.scalar_tensor_tensor(out=S2[:, 1 - u, :], in0=h_slot[u], scalar=LG, in1=S2[:, u, :],
                                           op0=ALU.mult, op1=ALU.add).then_inc(last_pick, 1)

                def body(r, s, first, final):
                    u = s % 2
                    dve.wait_ge(gates_tanh, 3 * r + 1)
                    v.scalar_tensor_tensor(out=w1b[:, :], in0=xp[:, D:2 * D], scalar=1.0, in1=c2[:, :],
                                           op0=ALU.add, op1=ALU.mult).then_inc(last_cell, 1)
                    dve.wait_ge(gates_tanh, 3 * r + 2)
                    v.scalar_tensor_tensor(out=xn[:, :], in0=xp[:, 0:D], scalar=1.0, in1=xp[:, 2 * D:3 * D],
                                           op0=ALU.add, op1=ALU.mult).then_inc(last_cell, 1)
                    dve.wait_ge(last_cell, 3 * r + 2)
                    v.scalar_tensor_tensor(out=c2[:, :], in0=w1b[:, :], scalar=0.5, in1=xn[:, :],
                                           op0=ALU.mult, op1=ALU.add).then_inc(last_cell, 1)
                    if not first:
                        dve.wait_ge(last_added, r)
                        hold(dve)
                    dve.wait_ge(last_cell_tanh, r + 1)
                    v.scalar_tensor_tensor(out=h_slot[u], in0=xp[:, 3 * D:G4], scalar=1.0, in1=w1[:, :],
                                           op0=ALU.add, op1=ALU.mult).then_inc(last_h, 1)
                    if not first:
                        dve.wait_ge(last_out, r)
                        hold(dve)
                        pick(r - 1, 1 - u)
                steps(dve, body)
                dve.wait_ge(last_out, WARM)
                hold(dve)
                pick(WARM - 1, 1)

            @block.gpsimd
            def _(pool):
                pool.sem_inc(last_pick, 3)
                pool.sem_inc(last_out, 1)
                pool.sem_inc(last_added, 1)
                nc.gpsimd.memset(strict, 1.0).then_inc(tables, 1)
                nc.gpsimd.memset(ones, 1.0).then_inc(tables, 1)
                pool.wait_ge(tables, 2)
                nc.gpsimd.affine_select(out=strict, in_=strict, compare_op=ALU.is_gt, fill=0.0,
                                        base=0, pattern=[[1, P]], channel_multiplier=-1).then_inc(tables, 1)

                def body(r, s, first, final):
                    u = s % 2
                    base_of = wh[:, bass.ds(r + OFF, 1), :].rearrange("k o d -> k (o d)")
                    pool.wait_ge(x1_back[s], loads(r, s))
                    hold(pool)
                    pool.wait_ge(last_pick, 3 * r + 6)
                    hold(pool)
                    nc.gpsimd.tensor_tensor(base_of, x1_slot[s], h_slot[u], ALU.add).then_inc(last_added, 1)
                    nc.gpsimd.tensor_tensor(w3[:, :], S2[:, u, :], fb[:, 0, :], ALU.mult).then_inc(last_part, 1)
                    pool.wait_ge(last_added, r + 2)
                    hold(pool)
                    pool.wait_ge(last_part, 3 * r + 1)
                    hold(pool)
                    nc.gpsimd.tensor_tensor(base_of, base_of, w3[:, :], ALU.add).then_inc(last_part, 1)
                    pool.wait_ge(last_part, 3 * r + 2)
                    nc.gpsimd.tensor_tensor(w3[:, :], S2[:, 1 - u, :], fb[:, 1, :], ALU.mult).then_inc(last_part, 1)
                    pool.wait_ge(last_part, 3 * r + 3)
                    hold(pool)
                    nc.gpsimd.tensor_tensor(base_of, base_of, w3[:, :], ALU.subtract).then_inc(last_out, 1)
                steps(pool, body)

        differ, differ_max, decided = sem("differ"), sem("differ_max"), sem("decided")
        with nc.Block() as block:
            @block.vector
            def _(dve):
                v = nc.vector
                v.tensor_tensor(x_in[:, 0, :], x_in[:, 0, :], h2[:, :], ALU.subtract)
                v.tensor_tensor(x_in[:, 1, :], x_in[:, 1, :], c2[:, :], ALU.subtract).then_inc(differ, 1)
                dve.wait_ge(differ, 1)
                v.tensor_reduce(out=DMX[:, 0:1], in_=x_in[:, :, :], axis=AX.XY, op=ALU.max,
                                apply_absolute_value=True).then_inc(differ, 1)
                dve.wait_ge(differ_max, 1)
                v.tensor_reduce(out=DMX[0:1, 1:2], in_=ps_x[0:1, 0:P], axis=AX.X, op=ALU.max).then_inc(differ, 1)
                dve.wait_ge(differ, 3)
                v.tensor_scalar(DMX[0:1, 2:3], DMX[0:1, 1:2], TOL, None, ALU.is_le).then_inc(differ, 1)
                dve.wait_ge(differ, 4)
                v.tensor_scalar(flag[0:1, 0:1], DMX[0:1, 2:3], -1.0, 1.0, ALU.mult, ALU.add).then_inc(decided, 1)

            @block.tensor
            def _(pe):
                pe.wait_ge(differ, 2)
                nc.tensor.matmul(ps_x[0:1, 0:P], DMX[:, 0:1], ident[:, :], start=True, stop=True).then_inc(differ_max, 1)

        g_load = sem("g_load")
        g_in, g_step, g_shift = sem("g_in"), sem("g_step"), sem("g_shift")
        g_start_h, g_start_c = sem("g_start_h"), sem("g_start_c")
        g_rec, g_sum, g_act, g_cell, g_cell_act = sem("g_rec"), sem("g_sum"), sem("g_act"), sem("g_cell"), sem("g_cell_act")
        g_h, g_hT_mm, g_hT, g_logit, g_base = sem("g_h"), sem("g_hT_mm"), sem("g_hT"), sem("g_logit"), sem("g_base")

        def sweeps(eng, start, step):
            needed = eng.value_load(flag[0:1, 0:1], min_val=0, max_val=1)
            with eng.If(needed):
                with eng.Fori(0, SWEEPS) as q:
                    start(q)
                    with eng.Fori(0, L) as l:
                        step(q * L + l, l)

        with nc.Block() as block:
            @block.sync
            def _(sp):
                def step(r, l):
                    sp.wait_ge(g_step, r + 1)
                    hold(sp)
                    sp.dma_start(xp_again, xp_dram[:, bass.ds(l, 1), :].rearrange("k o g -> k (o g)")).then_inc(g_load, 16)
                    sp.dma_start(x1_again, x1_dram[:, bass.ds(l, 1), :].rearrange("k o d -> k (o d)")).then_inc(g_load, 16)
                    sp.wait_ge(g_load, 32)
                    sp.sem_clear(g_load)
                    sp.sem_inc(g_in, 1)
                    sp.wait_ge(g_base, r + 1)
                    sp.sem_inc(g_step, 1)
                sp.sem_inc(g_step, 1)
                sweeps(sp, lambda q: None, step)

            @block.tensor
            def _(pe):
                def start(q):
                    pe.wait_ge(g_step, q * L + 1)
                    for k in range(KD):
                        nc.tensor.matmul(ps_h[:, k * P:(k + 1) * P], h2[:, k * P:(k + 1) * P], shift[:, :], start=True, stop=True)
                    nc.tensor.matmul(ps_x[:, D:2 * D], shift[:, :], c2[:, :], start=True, stop=True).then_inc(g_shift, 1)
                    pe.wait_ge(g_start_h, q + 1)
                    hold(pe)

                def step(r, l):
                    pe.wait_ge(g_step, r + 1)
                    for h in range(2):
                        for k in range(KD):
                            last = nc.tensor.matmul(ps_g[h][:, :], hT[:, k, :], whh[:, k, h * HALF:(h + 1) * HALF], start=k == 0, stop=k == KD - 1)
                    last.then_inc(g_rec, 1)
                    pe.wait_ge(g_h, r + 1)
                    for k in range(KD):
                        last = nc.tensor.transpose(ps_h[:, k * P:(k + 1) * P], h2[:, k * P:(k + 1) * P], ident[:, :])
                    last.then_inc(g_hT_mm, 1)
                    pe.wait_ge(g_hT, r + 1)
                    for k in range(KD):
                        last = nc.tensor.matmul(ps_h[:, 0:2], hT[:, k, :], wl[:, k, :], start=k == 0, stop=k == KD - 1)
                    last.then_inc(g_logit, 1)
                sweeps(pe, start, step)

            @block.scalar
            def _(act):
                def start(q):
                    act.wait_ge(g_shift, q + 1)
                    nc.scalar.copy(hT[:, :, :].rearrange("p k q -> p (k q)"), ps_h[:, 0:D]).then_inc(g_start_h, 1)

                def step(r, l):
                    act.wait_ge(g_sum, r + 1)
                    nc.scalar.activation(xp_again, xp_again, ACT.Tanh).then_inc(g_act, 1)
                    act.wait_ge(g_cell, r + 1)
                    nc.scalar.activation(w1[:, :], c2[:, :], ACT.Tanh, scale=0.5).then_inc(g_cell_act, 1)
                    act.wait_ge(g_hT_mm, r + 1)
                    nc.scalar.copy(hT[:, :, :].rearrange("p k q -> p (k q)"), ps_h[:, 0:D]).then_inc(g_hT, 1)
                sweeps(act, start, step)

            @block.vector
            def _(dve):
                v = nc.vector
                g = xp_again
                S = S2[:, 0, :]

                def start(q):
                    dve.wait_ge(g_shift, q + 1)
                    v.tensor_copy(c2[:, :], ps_x[:, D:2 * D])
                    v.memset(S, 0.0)
                    dve.drain()

                def step(r, l):
                    dve.wait_ge(g_in, r + 1)
                    hold(dve)
                    dve.wait_ge(g_rec, r + 1)
                    for h in range(2):
                        half = g[:, h * HALF:(h + 1) * HALF]
                        last = v.tensor_tensor(half, half, ps_g[h][:, :], ALU.add)
                    last.then_inc(g_sum, 1)
                    dve.wait_ge(g_act, r + 1)
                    v.scalar_tensor_tensor(out=w1b[:, :], in0=g[:, D:2 * D], scalar=1.0, in1=c2[:, :], op0=ALU.add, op1=ALU.mult)
                    v.scalar_tensor_tensor(out=xn[:, :], in0=g[:, 0:D], scalar=1.0, in1=g[:, 2 * D:3 * D], op0=ALU.add, op1=ALU.mult)
                    dve.drain()
                    v.scalar_tensor_tensor(out=c2[:, :], in0=w1b[:, :], scalar=0.5, in1=xn[:, :], op0=ALU.mult, op1=ALU.add).then_inc(g_cell, 1)
                    dve.wait_ge(g_cell_act, r + 1)
                    v.scalar_tensor_tensor(out=h2[:, :], in0=g[:, 3 * D:G4], scalar=1.0, in1=w1[:, :], op0=ALU.add, op1=ALU.mult).then_inc(g_h, 1)
                    dve.wait_ge(g_logit, r + 1)
                    v.tensor_scalar(LD, ps_h[:, 0:1], BL[:, 0:1], None, ALU.add)
                    v.tensor_tensor(base[:, :], x1_again, h2[:, :], ALU.add)
                    v.tensor_tensor(w2[:, :], S, fb[:, 0, :], ALU.mult)
                    dve.drain()
                    v.tensor_scalar(LG, ps_h[:, 1:2], BL[:, 1:2], LD, ALU.add, ALU.is_gt)
                    v.tensor_tensor(base[:, :], base[:, :], w2[:, :], ALU.add)
                    dve.drain()
                    v.scalar_tensor_tensor(out=S, in0=h2[:, :], scalar=LG, in1=S, op0=ALU.mult, op1=ALU.add)
                    dve.drain()
                    v.tensor_tensor(w2[:, :], S, fb[:, 1, :], ALU.mult)
                    dve.drain()
                    v.tensor_tensor(wh[:, bass.ds(l, 1), :].rearrange("k o d -> k (o d)"), base[:, :], w2[:, :],
                                    ALU.subtract).then_inc(g_base, 1)
                sweeps(dve, start, step)

        tot_mm, off_ready = sem("tot_mm"), sem("off_ready")
        out_ready, out_stored = sem("out_ready"), sem("out_stored")
        OB = 8
        OW = L // OB
        with nc.Block() as block:
            @block.tensor
            def _(pe):
                nc.tensor.matmul(ps_x[:, 0:D], strict, S2[:, 0, :], start=True, stop=True)
                nc.tensor.matmul(ps_h[:, 0:D], ones, S2[:, 0, :], start=True, stop=True).then_inc(tot_mm, 1)

            @block.sync
            def _(sp):
                for i in range(OB):
                    sp.wait_ge(out_ready, i + 1)
                    sp.dma_start(out_kl[:, i * OW:(i + 1) * OW, :], wh[:, i * OW:(i + 1) * OW, :]).then_inc(out_stored, 16)
                sp.wait_ge(out_stored, 16 * OB)

            @block.vector
            def _(dve):
                v = nc.vector
                dve.wait_ge(tot_mm, 1)
                v.tensor_copy(w1[:, :], ps_x[:, 0:D]).then_inc(off_ready, 1)
                dve.wait_ge(off_ready, 1)
                v.tensor_tensor(w2[:, :], ps_h[:, 0:D], w1[:, :], ALU.subtract).then_inc(off_ready, 1)
                v.tensor_tensor(w1[:, :], w1[:, :], fb[:, 0, :], ALU.mult).then_inc(off_ready, 1)
                dve.wait_ge(off_ready, 2)
                v.tensor_tensor(w2[:, :], w2[:, :], fb[:, 1, :], ALU.mult).then_inc(off_ready, 1)
                dve.wait_ge(off_ready, 4)
                v.tensor_tensor(w1[:, :], w1[:, :], w2[:, :], ALU.add).then_inc(off_ready, 1)
                dve.wait_ge(off_ready, 5)
                for i in range(OB):
                    part = wh[:, i * OW:(i + 1) * OW, :]
                    v.tensor_tensor(part, part, w1[:, :].rearrange("p (o d) -> p o d", o=1).to_broadcast([P, OW, D]),
                                    ALU.add).then_inc(out_ready, 1)


def kernel(x, adj, L0_gnn_W, L0_gnn_a, L0_ffn_W_ih, L0_ffn_W_hh, L0_ffn_b_ih, L0_ffn_b_hh, L0_ffn_W_lin,
           L0_ffn_b_lin, L0_ffn_fw_att, L0_ffn_bw_att):
    import numpy as np
    import concourse.bacc as bacc
    from concourse import mybir as mb
    from concourse.bass_utils import run_bass_kernel_spmd as run

    nc = bacc.Bacc("TRN2", target_bir_lowering=False, num_devices=1)
    laid = [("x", x), ("adj", adj), ("w_gnn", L0_gnn_W), ("a_pair", L0_gnn_a), ("w_ih_t", np.asarray(L0_ffn_W_ih).T),
            ("w_hh_t", np.asarray(L0_ffn_W_hh).T), ("b_ih", L0_ffn_b_ih), ("b_hh", L0_ffn_b_hh),
            ("w_lin_t", np.asarray(L0_ffn_W_lin).T), ("b_lin", L0_ffn_b_lin), ("fw", L0_ffn_fw_att), ("bw", L0_ffn_bw_att)]
    arrays, args = {}, []
    for name, a in laid:
        a = np.ascontiguousarray(a)
        arrays[name] = a
        args.append(nc.dram_tensor(name, a.shape, mb.dt.from_np(a.dtype), kind="ExternalInput").ap())
    args.append(nc.dram_tensor("out", x.shape, mb.dt.float32, kind="ExternalOutput").ap())
    adj_ffn_kernel(nc, *args)
    return run(nc, [arrays], core_ids=[0]).results[0]["out"]
```
